# Optimizing a Trainium2 kernel written in Bass

```python
import numpy as np
import jax
import jax.numpy as jnp

def _softmax(x, axis=-1):
    return jax.nn.softmax(x, axis=axis)
def _gelu(x):
    return jax.nn.gelu(x, approximate=True)
def _silu(x):
    return jax.nn.silu(x)
def _sigmoid(x):
    return jax.nn.sigmoid(x)
def _layernorm(x, axis=-1, eps=1e-5):
    m = jnp.mean(x, axis=axis, keepdims=True)
    v = jnp.var(x, axis=axis, keepdims=True)
    return (x - m) / jnp.sqrt(v + eps)
def _scatter_add(tgt, idx, src, axis=0):
    return tgt.at[idx].add(src)
def _segment_sum(src, seg, n):
    return jax.ops.segment_sum(src, seg, n)

kernel_name = 'mk_adj_preln_d2_adj_256_968a5a'

def setup_inputs(seed: int = 0):
    np.random.seed(seed)
    _w = jnp.asarray
    def _rec_inputs():
        import jax
        import jax.numpy as jnp
        _gk = jax.random.key(seed)
        x = -0.0002928 + 1 * jax.random.normal(jax.random.fold_in(_gk, 1), (8, 2048, 256), jnp.float32)
        _w = (1.0 + jnp.arange(2048, dtype=jnp.float32)) ** -0.5
        _w = _w / _w.mean()
        _pij = jnp.clip(0.00195312 * _w[:, None] * _w[None, :], 0.0, 1.0)
        _a = jax.random.uniform(jax.random.fold_in(_gk, 2), (8, 2048, 2048)) < _pij
        adj = _a.astype(jnp.int32)
        return x, adj
    x, adj = _rec_inputs()
    def _L0_gnn_setup():
        import jax, jax.numpy as jnp
        import numpy as np
        NEG_INF = -1000000000.0
        SLOPE = 0.2
        key = jax.random.key(seed)
        k1, k2, k3, k4 = jax.random.split(key, 4)
        B, N, Fin, Fout = (16, 1024, 256, 256)
        h = jax.random.normal(k1, (B, N, Fin), dtype=jnp.float32)
        adj = jax.random.randint(k2, (B, N, N), 0, 2, dtype=jnp.int32)
        W = jax.random.normal(k3, (Fin, Fout), dtype=jnp.float32) * (1.0 / np.sqrt(Fin))
        a = jax.random.normal(k4, (2 * Fout,), dtype=jnp.float32) * (1.0 / np.sqrt(2 * Fout))
        return {'h': h, 'adj': adj, 'W': W, 'a': a}
    _L0_gnn_all = _L0_gnn_setup()
    _L0_gnn_in = {k: v for k, v in _L0_gnn_all.items() if k in ('W', 'a', )}
    del _L0_gnn_all

    def _L1_gnn_setup():
        import jax, jax.numpy as jnp
        import numpy as np
        IN_F = 256
        OUT_F = 256
        ALPHA = 0.2

        def _xavier(key, shape, gain=1.414):
            fan_in, fan_out = (shape[0], shape[1])
            limit = gain * np.sqrt(6.0 / (fan_in + fan_out))
            return jax.random.uniform(key, shape, jnp.float32, -limit, limit)
        key = jax.random.key(seed)
        k1, k2, k3, k4 = jax.random.split(key, 4)
        B, N = (8, 2048)
        h = jax.random.normal(k1, (B, N, IN_F), jnp.float32)
        adj = jax.random.randint(k2, (B, N, N), 0, 2, jnp.int32)
        W = _xavier(k3, (IN_F, OUT_F))
        a = _xavier(k4, (2 * OUT_F, 1))
        return {'h': h, 'adj': adj, 'W': W, 'a': a}
    _L1_gnn_all = _L1_gnn_setup()
    _L1_gnn_in = {k: v for k, v in _L1_gnn_all.items() if k in ('W', 'a', )}
    del _L1_gnn_all

    return {
        "x": x,
        "adj": adj,
        "L0_gnn_W": _L0_gnn_in["W"],
        "L0_gnn_a": _L0_gnn_in["a"],
        "L1_gnn_W": _L1_gnn_in["W"],
        "L1_gnn_a": _L1_gnn_in["a"],
    }

def reference(x, adj, L0_gnn_W, L0_gnn_a, L1_gnn_W, L1_gnn_a):
    import jax
    import jax.numpy as jnp
    def _L0_gnn_ref(h, adj, W, a):
        import jax, jax.numpy as jnp
        import numpy as np
        NEG_INF = -1000000000.0
        SLOPE = 0.2
        Fout = W.shape[1]
        Wh = jnp.einsum('bnf,fo->bno', h, W)
        a1, a2 = (a[:Fout], a[Fout:])
        f1 = Wh @ a1
        f2 = Wh @ a2
        e = jax.nn.leaky_relu(f1[:, :, None] + f2[:, None, :], negative_slope=SLOPE)
        e = jnp.where(adj == 0, NEG_INF, e)
        attention = jax.nn.softmax(e, axis=-1)
        h_prime = jnp.einsum('bij,bjo->bio', attention, Wh)
        return h_prime

    def _L1_gnn_ref(h, adj, W, a):
        import jax, jax.numpy as jnp
        import numpy as np
        IN_F = 256
        OUT_F = 256
        ALPHA = 0.2

        def _xavier(key, shape, gain=1.414):
            fan_in, fan_out = (shape[0], shape[1])
            limit = gain * np.sqrt(6.0 / (fan_in + fan_out))
            return jax.random.uniform(key, shape, jnp.float32, -limit, limit)
        Wh = jnp.einsum('bni,io->bno', h, W)
        a1 = a[:OUT_F, 0]
        a2 = a[OUT_F:, 0]
        e1 = Wh @ a1
        e2 = Wh @ a2
        e = e1[:, :, None] + e2[:, None, :]
        e = jnp.where(e > 0, e, ALPHA * e)
        neg = jnp.float32(-9000000000000000.0)
        scores = jnp.where(adj > 0, e, neg)
        attention = jax.nn.softmax(scores, axis=2)
        h_prime = jnp.einsum('bnm,bmo->bno', attention, Wh)
        return jax.nn.elu(h_prime)

    h = jnp.maximum(_layernorm(x, axis=-1), 0.0)
    x = x + _L0_gnn_ref(h, adj, L0_gnn_W, L0_gnn_a)
    h = jnp.maximum(_layernorm(x, axis=-1), 0.0)
    x = x + _L1_gnn_ref(h, adj, L1_gnn_W, L1_gnn_a)
    return x


_drawn_inputs = setup_inputs


def setup_inputs(seed=0):
    import zlib

    import numpy as np

    out = dict(_drawn_inputs(seed))
    spreads = {}
    factors = {}
    for name, (base, spread) in spreads.items():
        noise = np.random.default_rng([zlib.crc32(name.encode()), seed]).standard_normal(out[name].shape)
        drawn = base * np.exp(spread * noise) if base else spread * noise
        out[name] = jnp.asarray(drawn.astype(out[name].dtype))
    for name, factor in factors.items():
        out[name] = (out[name] * factor).astype(out[name].dtype)
    return out
```

```python
from contextlib import ExitStack

import concourse.bass as bass
from concourse import mybir
from concourse.alu_op_type import AluOpType as ALU


F32 = mybir.dt.float32
F32R = mybir.dt.float32r
BF16 = mybir.dt.bfloat16
U8 = mybir.dt.uint8
ACT = mybir.ActivationFunctionType
AX = mybir.AxisListType.X

P = 128
SLOPE = 0.2
EPS = 1e-5
FLOOR = -80.0


class Phase:

    def __init__(self, p, odd, layer, graph, parity):
        self.p, self.odd, self.layer, self.graph, self.parity = p, odd, layer, graph, parity
        self.prev = self.next = None
        self.late_adj = None
        self.early_adj = None


def gat_kernel(nc, x, adj, w_l0, a_l0, w_l1, a_l1, out):
    B, N, F = x.shape
    T = N // P
    CH = 512
    NC = N // CH
    TC = CH // P
    NQ = T // 2
    STEPS = NC * NQ
    K2 = F // P
    FW = F + 2
    FV = F + 1
    XS = 2
    NS = 2

    TILE_AT = {1 + (5 * t) // 4: t for t in range(T)}
    STEP_OF = {t: s for s, t in TILE_AT.items()}
    REDUCE_AT = STEP_OF[T - 1] + 2
    FACTOR_AT = REDUCE_AT + 1
    EXP_AT = FACTOR_AT + 2
    SPREAD_AT = EXP_AT + 1
    VALUES_AT = STEPS - NQ + 3

    assert 3 * NQ <= SPREAD_AT < STEPS and EXP_AT < VALUES_AT

    scratch = nc.dram_tensor("beta_rows", (T, P), F32).ap()
    adj_rows = adj.rearrange("b (t p) j -> b t p j", p=P)
    x_rows = x.rearrange("b (t p) f -> b p t f", p=P)
    out_rows = out.rearrange("b (t p) f -> b p t f", p=P)

    ctx = ExitStack()
    with ctx:
        def sb(name, shape, dt=F32):
            return ctx.enter_context(nc.sbuf_tensor(name, shape, dt))

        def pb(name, shape, dt=F32):
            return ctx.enter_context(nc.psum_tensor(name, shape, dt))

        def sem(name):
            return ctx.enter_context(nc.semaphore(name))

        adj_t = sb("adj_t", [P, 2, T, N], U8)
        adj_in = sb("adj_in", [P, NS, N], BF16)
        xres = sb("xres", [P, 2, T, F])
        x_in = sb("x_in", [P, XS, F])
        hrow = sb("hrow", [P, 2, F])
        hcol = sb("hcol", [P, 2, K2, P])
        wh = sb("wh", [P, T, FW])
        v_hi = sb("v_hi", [P, T, FW], F32R)
        v_lo = sb("v_lo", [P, T, FW], F32R)
        beta_b = sb("beta_b", [P, N])
        g_full = sb("g_full", [P, 2, 2, CH])
        g_hi = sb("g_hi", [P, 2, 2, CH], F32R)
        g_lo = sb("g_lo", [P, 2, 2, CH], F32R)
        wcat = sb("wcat", [P, 2, K2, FW])
        ident_f = sb("ident_f", [P, P])
        ident_b = sb("ident_b", [P, P], BF16)
        ones = sb("ones", [P, P])
        hmean_b = sb("hmean_b", [P, K2, P])
        wh_mean = sb("wh_mean", [P, 2, FV])
        acc_sb = sb("acc_sb", [P, TC, FW])
        expy = sb("expy", [P, 2, F])
        beta_r = sb("beta_r", [T, P])
        stat = sb("stat", [P, 8, 6])
        moment = sb("moment", [P, 8, 2])
        vareps = sb("vareps", [P, 8])
        rstd = sb("rstd", [P, 8])
        shift = sb("shift", [P, 8])
        scaled = sb("scaled", [P, 8])
        minus_half = sb("minus_half", [P, 1])
        eps = sb("eps", [P, 1])
        zero = sb("zero", [P, 1])
        hsum = sb("hsum", [P, K2, T])
        htot = sb("htot", [P, K2])
        fmax = sb("fmax", [P, 1])
        fmax_top = sb("fmax_top", [1, 1])
        fmax_all = sb("fmax_all", [P, 1])
        f2_rel = sb("f2_rel", [P, T])
        f1_top = sb("f1_top", [P, T])
        r_col = sb("r_col", [P, 2, T])
        v_col = sb("v_col", [P, T])
        beta_c = sb("beta_c", [P, T])
        alone = sb("alone", [P, TC])
        rden = sb("rden", [P, TC])

        acc = [pb(f"acc{t}", [P, 512]) for t in range(TC)]
        ps_h = pb("ps_h", [P, K2, P + P])
        ps_w = pb("ps_w", [P, 512])
        ps_a = [pb(f"ps_a{h}", [P, NQ, P], BF16) for h in range(2)]

        setup_dma = sem("setup_dma")
        consts_made = sem("consts_made")
        wcat_made = sem("wcat_made")
        vconst_made = sem("vconst_made")
        x_loaded = [sem(f"x_loaded{i}") for i in range(XS)]
        adj_loaded = [sem(f"adj_loaded{i}") for i in range(NS)]
        res_loaded = [sem(f"res_loaded{c}") for c in range(NC)]
        out_stored = [sem(f"out_stored{c}") for c in range(NC)]
        adj_turned = sem("adj_turned")
        adj_kept = sem("adj_kept")
        stats_made = sem("stats_made")
        moments_made = sem("moments_made")
        rstd_steps = sem("rstd_steps")
        h_made = sem("h_made")
        h_turned = sem("h_turned")
        hcol_made = sem("hcol_made")
        wh_done = sem("wh_done")
        wh_kept = sem("wh_kept")
        reduced = sem("reduced")
        fmax_turned = sem("fmax_turned")
        top_made = sem("top_made")
        top_spread = sem("top_spread")
        fmax_made = sem("fmax_made")
        args_made = sem("args_made")
        one_made = sem("one_made")
        factors_made = sem("factors_made")
        hmean_made = sem("hmean_made")
        beta_turned = sem("beta_turned")
        mean_done = sem("mean_done")
        beta_kept = sem("beta_kept")
        mean_kept = sem("mean_kept")
        beta_stored = sem("beta_stored")
        beta_in_012 = sem("beta_in_012")
        beta_in_3 = sem("beta_in_3")
        v_hi_made = sem("v_hi_made")
        v_lo_made = sem("v_lo_made")
        g_made = sem("g_made")
        g_hi_made = sem("g_hi_made")
        g_lo_made = sem("g_lo_made")
        step_done = sem("step_done")
        acc_done = sem("acc_done")
        acc_kept = sem("acc_kept")
        fix_steps = sem("fix_steps")
        x1_made = sem("x1_made")
        elu_parts = sem("elu_parts")
        elu_half = sem("elu_half")
        out_made = sem("out_made")

        block = ctx.enter_context(nc.Block())

        def wait(eng, semaphore, value):
            if isinstance(value, int) and value <= 0:
                return
            eng.wait_ge(semaphore, value)

        def make(p, odd, layer, graph):
            return Phase(p, odd, layer, graph, graph % 2)

        def opening():
            a, b, c = make(0, 0, 0, 0), make(1, 1, 0, 1), make(2, 0, 1, 0)
            a.next, b.prev, b.next, c.prev = b, a, c, b
            a.early_adj, a.late_adj = 0, 1
            b.early_adj = 1
            return [a, b]

        def middle(r):
            a, b = make(2 * r, 0, 1, r - 1), make(2 * r + 1, 1, 0, r + 1)
            a.prev, a.next, b.prev = make(2 * r - 1, 1, 0, r), b, a
            b.next = make(2 * r + 2, 0, 1, r)
            a.late_adj, b.early_adj = r + 1, r + 1
            return [a, b]

        def closing():
            a, b = make(2 * B - 2, 0, 1, B - 2), make(2 * B - 1, 1, 1, B - 1)
            a.prev, a.next, b.prev = make(2 * B - 3, 1, 0, B - 1), b, a
            return [a, b]

        def program(eng, phase):
            for ph in opening():
                phase(ph)
            with eng.Fori(1, B - 1) as r:
                for ph in middle(r):
                    phase(ph)
            for ph in closing():
                phase(ph)

        def adj_jobs(ph, s):
            if ph.early_adj is not None and s < 16 and s % 2 == 0:
                return [(ph.early_adj, T // 2 + s // 2)]
            if ph.late_adj is not None and s >= 16 and s % 2 == 0:
                return [(ph.late_adj, (s - 16) // 2)]
            return []

        def before(ph, c):
            return (ph, c - 1) if c else (ph.prev, NC - 1)

        @block.sync
        def _(sp):
            for n, (w, a) in enumerate(((w_l0, a_l0), (w_l1, a_l1))):
                with nc.allow_non_contiguous_dma(reason="rows of W and both halves of a for all partitions"):
                    sp.dma_start(wcat[:, n, :, 0:F], w.rearrange("(k p) o -> p k o", p=P)).then_inc(setup_dma, 16)
                    sp.dma_start(g_full[:, 0, n, :], a.partition_broadcast(P)).then_inc(setup_dma, 16)

            def x_tile(n, graph, t):
                j = 16 * n + t
                wait(sp, h_made, j - XS + 1)
                sp.dma_start(x_in[:, t % XS, :], x_rows[graph, :, t, :]).then_inc(x_loaded[t % XS], 16)

            def residual(graph, parity, c):
                if not (isinstance(graph, int) and graph < 2):
                    sp.wait_ge(out_stored[c], 16 * (graph - 1))
                    sp.wait_ge(out_made, 16 * (graph - 2) + 4 * c + 4)
                sp.dma_start(xres[:, parity, TC * c:TC * c + TC, :],
                             x_rows[graph, :, TC * c:TC * c + TC, :]).then_inc(res_loaded[c], 16)

            def store(graph, parity, c):
                sp.wait_ge(out_made, 16 * graph + 4 * c + 4)
                sp.dma_start(out_rows[graph, :, TC * c:TC * c + TC, :],
                             xres[:, parity, TC * c:TC * c + TC, :]).then_inc(out_stored[c], 16)

            def beta(n):
                sp.wait_ge(beta_kept, n + 1)
                sp.dma_start(scratch, beta_r[:, :]).then_inc(beta_stored, 16)
                sp.wait_ge(beta_stored, 16 * (n + 1))
                lot = 3 * TC
                sp.dma_start(beta_b[:, 0:lot * P],
                             scratch[0:lot, :].rearrange("t p -> (t p)").partition_broadcast(P)).then_inc(beta_in_012, 16)

            def beta_rest(n):
                wait(sp, g_made, STEPS * n)
                lot = 3 * TC
                sp.dma_start(beta_b[:, lot * P:N],
                             scratch[lot:T, :].rearrange("t p -> (t p)").partition_broadcast(P)).then_inc(beta_in_3, 16)

            def phase(ph):
                nxt = ph.next
                if ph.layer == 0:
                    for c in range(NC - 1):
                        residual(ph.graph, ph.parity, c)
                if ph.prev is not None and ph.prev.layer == 1:
                    store(ph.prev.graph, ph.prev.parity, NC - 1)
                if ph.layer == 0:
                    residual(ph.graph, ph.parity, NC - 1)
                if nxt is not None and nxt.layer == 0:
                    for t in range(T):
                        x_tile(nxt.p, nxt.graph, t)
                if ph.layer == 1:
                    store(ph.graph, ph.parity, 0)
                if nxt is not None:
                    beta(nxt.p)
                if ph.layer == 1:
                    store(ph.graph, ph.parity, 1)
                    if nxt is None:
                        store(ph.graph, ph.parity, 2)
                if nxt is not None:
                    beta_rest(nxt.p)
                if ph.layer == 1 and nxt is not None:
                    store(ph.graph, ph.parity, 2)

            for t in range(T):
                x_tile(0, 0, t)
            beta(0)
            beta_rest(0)
            program(sp, phase)
            store(B - 1, (B - 1) % 2, NC - 1)
            for c in range(NC):
                sp.wait_ge(out_stored[c], 16 * B)

        @block.gpsimd
        def _(pool):
            def adj_load(graph, t):
                j = 16 * graph + t
                wait(pool, adj_turned, 2 * (j - NS) + 2)
                pool.dma_start(adj_in[:, t % NS, :], adj_rows[graph, t, :, :]).then_inc(adj_loaded[t % NS], 16)

            adj_load(0, 0)
            adj_load(0, 1)
            nc.gpsimd.memset(ones[:], 1.0)
            nc.gpsimd.memset(minus_half[:], -0.5)
            nc.gpsimd.memset(eps[:], EPS)
            nc.gpsimd.memset(zero[:], 0.0)
            nc.gpsimd.memset(ident_f[:], 0.0).then_inc(consts_made, 1)
            pool.wait_ge(consts_made, 1)
            nc.gpsimd.affine_select(out=ident_f[:], in_=ident_f[:], compare_op=ALU.not_equal, fill=1.0, base=0,
                                    pattern=[[-1, P]], channel_multiplier=1).then_inc(consts_made, 1)
            pool.wait_ge(consts_made, 2)
            nc.gpsimd.tensor_copy(ident_b[:], ident_f[:]).then_inc(consts_made, 1)
            pool.wait_ge(consts_made, 3)

            def tile_rstd(n, t):
                j, q = 16 * n + t, t % 8
                pool.wait_ge(moments_made, j + 1)
                wait(pool, h_made, j - 7)
                col = slice(q, q + 1)
                nc.gpsimd.tensor_tensor(vareps[:, col], moment[:, q, 1:2], eps[:], ALU.add).then_inc(rstd_steps, 1)
                pool.wait_ge(rstd_steps, 4 * j + 1)
                nc.gpsimd.tensor_tensor(rstd[:, col], vareps[:, col], minus_half[:], ALU.pow).then_inc(rstd_steps, 1)
                pool.wait_ge(rstd_steps, 4 * j + 2)
                nc.gpsimd.tensor_tensor(scaled[:, col], moment[:, q, 0:1], rstd[:, col],
                                        ALU.mult).then_inc(rstd_steps, 1)
                pool.wait_ge(rstd_steps, 4 * j + 3)
                nc.gpsimd.tensor_tensor(shift[:, col], zero[:], scaled[:, col], ALU.subtract).then_inc(rstd_steps, 1)

            def phase(ph):
                for s in range(STEPS):
                    for graph, t in adj_jobs(ph, s):
                        adj_load(graph, t)
                    if ph.next is not None and s in TILE_AT:
                        tile_rstd(ph.next.p, TILE_AT[s])

            for t in range(T):
                tile_rstd(0, t)
                if NS <= t + NS < T // 2:
                    adj_load(0, t + NS)
            program(pool, phase)

        @block.vector
        def _(dve):
            def edge_weights(ph, c, q):
                k = STEPS * ph.p + NQ * c + q
                if q == 0:
                    dve.wait_ge(adj_kept, 32 * ph.graph + 8 * c + 8)
                    dve.wait_ge(beta_in_012 if c < NC - 1 else beta_in_3, 16 * (ph.p + 1))
                    dve.wait_ge(factors_made, ph.p + 1)
                wait(dve, g_hi_made, k - 1)
                wait(dve, g_lo_made, k - 1)
                for i in range(2):
                    kt = 2 * q + i
                    ins = nc.vector.scalar_tensor_tensor(
                        out=g_full[:, q % 2, i, :], in0=beta_b[:, CH * c:CH * c + CH],
                        scalar=r_col[:, ph.odd, kt:kt + 1], in1=adj_t[:, ph.parity, kt, CH * c:CH * c + CH],
                        op0=ALU.max, op1=ALU.mult)
                ins.then_inc(g_made, 1)

            def edge_rest(ph, c, q):
                k = STEPS * ph.p + NQ * c + q
                dve.wait_ge(g_hi_made, k + 1)
                wait(dve, step_done, k - 1)
                nc.vector.tensor_tensor(g_lo[:, q % 2, :, :], g_full[:, q % 2, :, :],
                                        g_hi[:, q % 2, :, :].bitcast(F32), ALU.subtract).then_inc(g_lo_made, 1)

            def rows_ready(ph, t):
                if ph.layer == 0:
                    dve.wait_ge(x_loaded[t % XS], 16 * (8 * ph.graph + t // 2 + 1))
                else:
                    dve.wait_ge(x1_made, 16 * ph.graph + t + 1)
                wait(dve, rstd_steps, 4 * (16 * ph.p + t - 7))

            def tile_stats(ph, t):
                src = x_in[:, t % XS, :] if ph.layer == 0 else xres[:, ph.parity, t, :]
                nc.vector.bn_stats(stat[:, t % 8, :], src).then_inc(stats_made, 1)

            def stats_ready(ph, t):
                dve.wait_ge(stats_made, 16 * ph.p + t + 1)

            def tile_moments(t):
                nc.vector.bn_aggr(moment[:, t % 8, :], stat[:, t % 8, :]).then_inc(moments_made, 1)

            def reduce(n):
                dve.wait_ge(wh_kept, 16 * n + 16)
                nc.vector.tensor_reduce(out=htot[:], in_=hsum[:, :, :], axis=AX, op=ALU.add).then_inc(reduced, 1)
                nc.vector.tensor_reduce(out=fmax[:], in_=wh[:, :, F + 1], axis=AX, op=ALU.max).then_inc(reduced, 1)

            def top(n):
                dve.wait_ge(fmax_turned, n + 1)
                nc.vector.tensor_reduce(out=fmax_top[:], in_=ps_w[0:1, 0:P], axis=AX, op=ALU.max).then_inc(top_made, 1)

            def arguments(n):
                dve.wait_ge(top_spread, n + 1)
                nc.vector.tensor_copy(fmax_all[:], ps_w[:, P:P + 1]).then_inc(fmax_made, 1)
                dve.wait_ge(fmax_made, n + 1)
                nc.vector.tensor_scalar(f2_rel[:], wh[:, :, F + 1], fmax_all[:], FLOOR,
                                        ALU.subtract, ALU.max).then_inc(args_made, 1)
                nc.vector.tensor_scalar(f1_top[:], wh[:, :, F], fmax_all[:], 0.0,
                                        ALU.add, ALU.max).then_inc(args_made, 1)
                dve.wait_ge(args_made, 2 * n + 2)
                nc.vector.memset(wh[:, :, F:F + 1], 1.0).then_inc(one_made, 1)

            def values_rest(n, m):
                for kt in (2 * m, 2 * m + 1):
                    dve.wait_ge(v_hi_made, 16 * n + kt + 1)
                    nc.vector.scalar_tensor_tensor(
                        out=v_lo[:, kt, 0:FV], in0=wh[:, kt, 0:FV], scalar=v_col[:, kt:kt + 1],
                        in1=v_hi[:, kt, 0:FV].bitcast(F32), op0=ALU.mult, op1=ALU.subtract).then_inc(v_lo_made, 1)

            def chunk_end(ph, c, q):
                k = NC * ph.p + c
                if q == 0:
                    dve.wait_ge(acc_kept, 4 * k + 4)
                    nc.vector.tensor_scalar(alone[:], acc_sb[:, :, F + 1], 0.0, None,
                                            ALU.is_equal).then_inc(fix_steps, 1)
                if q in (1, 2):
                    if q == 1:
                        dve.wait_ge(fix_steps, 6 * k + 1)
                        dve.wait_ge(mean_kept, ph.p + 1)
                    for t in (2 * q - 2, 2 * q - 1):
                        nc.vector.scalar_tensor_tensor(
                            out=acc_sb[:, t, 0:FV], in0=wh_mean[:, ph.odd, :], scalar=alone[:, t:t + 1],
                            in1=acc_sb[:, t, 0:FV], op0=ALU.mult, op1=ALU.add).then_inc(fix_steps, 1)
                if q == 2:
                    dve.wait_ge(fix_steps, 6 * k + 5)
                    nc.vector.reciprocal(rden[:], acc_sb[:, :, F]).then_inc(fix_steps, 1)
                if q in (3, 4) and ph.layer == 0:
                    if q == 3:
                        dve.wait_ge(fix_steps, 6 * k + 6)
                        dve.wait_ge(res_loaded[c], 16 * (ph.graph + 1))
                    for t in (2 * q - 6, 2 * q - 5):
                        row = xres[:, ph.parity, TC * c + t, :]
                        nc.vector.scalar_tensor_tensor(out=row, in0=acc_sb[:, t, 0:F], scalar=rden[:, t:t + 1],
                                                       in1=row, op0=ALU.mult, op1=ALU.add).then_inc(x1_made, 1)
                if q in (4, 6) and ph.layer == 1:
                    lot = (q - 4, q - 3)
                    j = 16 * ph.graph + 4 * c
                    for t in lot:
                        dve.wait_ge(elu_parts, j + t + 1)
                        e = expy[:, t % 2, :]
                        nc.vector.scalar_tensor_tensor(out=e, in0=e, scalar=1.0, in1=acc_sb[:, t, 0:F],
                                                       op0=ALU.min, op1=ALU.add).then_inc(elu_half, 1)
                    for t in lot:
                        dve.wait_ge(elu_half, j + t + 1)
                        row = xres[:, ph.parity, TC * c + t, :]
                        nc.vector.scalar_tensor_tensor(out=row, in0=expy[:, t % 2, :], scalar=-1.0, in1=row,
                                                       op0=ALU.add, op1=ALU.add).then_inc(out_made, 1)

            def phase(ph):
                for s in range(STEPS):
                    c, q = s // NQ, s % NQ
                    has_tile = ph.next is not None and s + 1 in TILE_AT
                    if has_tile:
                        rows_ready(ph.next, TILE_AT[s + 1])
                    if s + 1 < STEPS:
                        edge_weights(ph, (s + 1) // NQ, (s + 1) % NQ)
                    elif ph.next is not None:
                        edge_weights(ph.next, 0, 0)
                    if has_tile:
                        tile_stats(ph.next, TILE_AT[s + 1])
                        stats_ready(ph.next, TILE_AT[s + 1])
                    edge_rest(ph, c, q)
                    if has_tile:
                        tile_moments(TILE_AT[s + 1])
                    late, at = before(ph, c)
                    if late is not None:
                        chunk_end(late, at, q)
                    if s < 3:
                        if ph.prev is not None:
                            values_rest(ph.p, 5 + s)
                    if ph.next is not None:
                        if s == REDUCE_AT:
                            reduce(ph.next.p)
                        if s == FACTOR_AT:
                            top(ph.next.p)
                        if s == FACTOR_AT + 1:
                            arguments(ph.next.p)
                        if s >= VALUES_AT:
                            values_rest(ph.next.p, s - VALUES_AT)

            dve.wait_ge(setup_dma, 64)
            for n in range(2):
                for k in range(K2):
                    for i in range(2):
                        ins = nc.vector.tensor_tensor_reduce(
                            out=g_full[:, 1, n, F * i:F * i + F], in0=wcat[:, n, k, 0:F],
                            in1=g_full[:, 0, n, F * i:F * i + F], scale=1.0, scalar=0.0, op0=ALU.mult, op1=ALU.add,
                            accum_out=wcat[:, n, k, F + i:F + i + 1])
                        ins.then_inc(wcat_made, 1)
                        dve.wait_ge(wcat_made, 4 * n + 2 * k + i + 1)
            nc.vector.memset(v_hi[:, :, F + 1:F + 2].bitcast(F32), 1.0)
            nc.vector.memset(v_lo[:, :, F + 1:F + 2].bitcast(F32), 0.0)
            nc.vector.memset(wh_mean[:, :, F:F + 1], 1.0).then_inc(vconst_made, 1)
            dve.wait_ge(vconst_made, 1)
            first = opening()[0]
            for t in range(T):
                rows_ready(first, t)
                tile_stats(first, t)
                stats_ready(first, t)
                tile_moments(t)
            reduce(0)
            top(0)
            arguments(0)
            for m in range(NQ):
                values_rest(0, m)
            edge_weights(first, 0, 0)
            program(dve, phase)
            last = closing()[1]
            for q in range(NQ):
                chunk_end(last, NC - 1, q)

        @block.scalar
        def _(act):
            def adj_keep(graph, t):
                j = 16 * graph + t
                for h in range(2):
                    act.wait_ge(adj_turned, 2 * j + h + 1)
                    nc.scalar.activation(adj_t[:, graph % 2, NQ * h:NQ * h + NQ, P * t:P * t + P], ps_a[h][:, :, :],
                                         ACT.Copy).then_inc(adj_kept, 1)

            def tile_normalise(ph, t):
                j, q = 16 * ph.p + t, t % 8
                act.wait_ge(rstd_steps, 4 * j + 4)
                wait(act, h_turned, j - 1)
                src = x_in[:, t % XS, :] if ph.layer == 0 else xres[:, ph.parity, t, :]
                nc.scalar.activation(hrow[:, t % 2, :], src, ACT.Relu, bias=shift[:, q:q + 1],
                                     scale=rstd[:, q:q + 1]).then_inc(h_made, 1)

            def tile_columns(ph, t):
                j = 16 * ph.p + t
                act.wait_ge(h_turned, j + 1)
                wait(act, wh_done, j - 1)
                if t == 0:
                    wait(act, reduced, 2 * ph.p)
                for k in range(K2):
                    ins = nc.scalar.activation(hcol[:, t % 2, k, :], ps_h[:, k, 0:P], ACT.Copy,
                                               accum_out=hsum[:, k, t:t + 1])
                ins.then_inc(hcol_made, 1)

            def tile_keep(ph, t):
                j = 16 * ph.p + t
                act.wait_ge(wh_done, j + 1)
                wait(act, v_lo_made, j - 15)
                nc.scalar.activation(wh[:, t, :], ps_w[:, 0:FW], ACT.Copy).then_inc(wh_kept, 1)

            def factors(ph):
                n = ph.p
                act.wait_ge(args_made, 2 * n + 2)
                nc.scalar.activation(r_col[:, ph.odd, :], f2_rel[:], ACT.Exp, scale=1.0 - SLOPE)
                nc.scalar.activation(v_col[:], f2_rel[:], ACT.Exp, scale=SLOPE)
                nc.scalar.activation(beta_c[:], f1_top[:], ACT.Exp, scale=SLOPE - 1.0).then_inc(factors_made, 1)
                act.wait_ge(reduced, 2 * n + 2)
                for k in range(K2):
                    ins = nc.scalar.activation(hmean_b[:, k, :], ones[:], ACT.Copy, scale=htot[:, k:k + 1])
                ins.then_inc(hmean_made, 1)

            def spread(ph):
                n = ph.p
                act.wait_ge(beta_turned, n + 1)
                wait(act, beta_stored, 16 * n)
                nc.scalar.activation(beta_r[:], ps_w[0:T, 0:P], ACT.Copy).then_inc(beta_kept, 1)
                act.wait_ge(mean_done, n + 1)
                nc.scalar.activation(wh_mean[:, ph.odd, 0:F], ps_h[:, 0, 0:F], ACT.Copy,
                                     scale=1.0 / N).then_inc(mean_kept, 1)

            def values_high(n, m):
                act.wait_ge(one_made, n + 1)
                act.wait_ge(factors_made, n + 1)
                wait(act, step_done, STEPS * (n - 1) + 3 * NQ + m + 1 if not (isinstance(n, int) and n == 0) else 0)
                for kt in (2 * m, 2 * m + 1):
                    nc.scalar.activation(v_hi[:, kt, 0:FV], wh[:, kt, 0:FV], ACT.Copy,
                                         scale=v_col[:, kt:kt + 1]).then_inc(v_hi_made, 1)

            def edge_high(ph, c, q):
                k = STEPS * ph.p + NQ * c + q
                act.wait_ge(g_made, k + 1)
                wait(act, step_done, k - 1)
                nc.scalar.activation(g_hi[:, q % 2, :, :], g_full[:, q % 2, :, :], ACT.Copy).then_inc(g_hi_made, 1)

            def acc_keep(ph, c):
                k = NC * ph.p + c
                late, at = before(ph, c)
                if late is not None:
                    act.wait_ge(out_made if late.layer else x1_made, 16 * late.graph + 4 * at + 4)
                for t in range(TC):
                    if t < TC - 1:
                        act.wait_ge(acc_done, 3 * k + t + 1)
                    else:
                        act.wait_ge(step_done, NQ * (k + 1))
                    nc.scalar.activation(acc_sb[:, t, :], acc[t][:, 0:FW], ACT.Copy).then_inc(acc_kept, 1)

            def elu(ph, c, q):
                k = NC * ph.p + c
                j = 16 * ph.graph + 4 * c
                act.wait_ge(fix_steps, 6 * k + 6)
                for t in (q - 3, q - 2):
                    if t >= 2:
                        act.wait_ge(out_made, j + t - 1)
                    nc.scalar.activation(expy[:, t % 2, :], acc_sb[:, t, 0:F], ACT.Exp, scale=rden[:, t:t + 1])
                    nc.scalar.activation(acc_sb[:, t, 0:F], acc_sb[:, t, 0:F], ACT.Relu,
                                         scale=rden[:, t:t + 1]).then_inc(elu_parts, 1)

            def phase(ph):
                for s in range(STEPS):
                    c, q = s // NQ, s % NQ
                    late, at = before(ph, c)
                    if q == 0 and late is not None:
                        acc_keep(late, at)
                    if ph.next is not None and s - 1 in TILE_AT:
                        tile_keep(ph.next, TILE_AT[s - 1])
                    if ph.next is not None and s in TILE_AT:
                        tile_normalise(ph.next, TILE_AT[s])
                    if s + 1 < STEPS:
                        edge_high(ph, (s + 1) // NQ, (s + 1) % NQ)
                    elif ph.next is not None:
                        edge_high(ph.next, 0, 0)
                    if ph.next is not None and s in TILE_AT:
                        tile_columns(ph.next, TILE_AT[s])
                    if late is not None and late.layer == 1 and q in (3, 5):
                        elu(late, at, q)
                    for graph, t in adj_jobs(ph, s):
                        adj_keep(graph, t)
                    if s < 3 and ph.prev is not None:
                        values_high(ph.p, 5 + s)
                    if ph.next is not None:
                        if s == EXP_AT:
                            factors(ph.next)
                        if s == SPREAD_AT:
                            spread(ph.next)
                        if s >= VALUES_AT:
                            values_high(ph.next.p, s - VALUES_AT)

            first = opening()[0]
            for t in range(T):
                tile_normalise(first, t)
                tile_columns(first, t)
                tile_keep(first, t)
                if t < T // 2:
                    adj_keep(0, t)
            factors(first)
            spread(first)
            for m in range(NQ):
                values_high(0, m)
            edge_high(first, 0, 0)
            program(act, phase)
            last = closing()[1]
            acc_keep(last, NC - 1)
            for q in (3, 5):
                elu(last, NC - 1, q)

        @block.tensor
        def _(pe):
            def adj_turn(graph, t, h):
                j = 16 * graph + t
                if h == 0:
                    pe.wait_ge(adj_loaded[t % NS], 16 * (8 * graph + t // 2 + 1))
                wait(pe, adj_kept, 2 * j + h - 1)
                for i in range(NQ):
                    kt = NQ * h + i
                    ins = nc.tensor.transpose(ps_a[h][:, i, :], adj_in[:, t % NS, P * kt:P * kt + P], ident_b[:])
                ins.then_inc(adj_turned, 1)

            def tile_turn(n, t):
                j = 16 * n + t
                pe.wait_ge(h_made, j + 1)
                wait(pe, hcol_made, j)
                if t == 0:
                    wait(pe, mean_kept, n)
                for k in range(K2):
                    ins = nc.tensor.transpose(ps_h[:, k, 0:P], hrow[:, t % 2, P * k:P * k + P], ident_f[:])
                ins.then_inc(h_turned, 1)

            def tile_project(ph, t):
                n = ph.p
                j = 16 * n + t
                pe.wait_ge(hcol_made, j + 1)
                wait(pe, wh_kept, j)
                if t == 0:
                    wait(pe, beta_kept, n)
                for k in range(K2):
                    ins = nc.tensor.matmul(ps_w[:, 0:FW], hcol[:, t % 2, k, :], wcat[:, ph.layer, k, :],
                                           start=(k == 0), stop=(k == K2 - 1))
                ins.then_inc(wh_done, 1)

            def maximum_turn(n):
                pe.wait_ge(reduced, 2 * n + 2)
                nc.tensor.transpose(ps_w[0:1, 0:P], fmax[:], ident_f[:]).then_inc(fmax_turned, 1)

            def maximum_spread(n):
                pe.wait_ge(top_made, n + 1)
                nc.tensor.matmul(ps_w[:, P:P + 1], ones[0:1, :], fmax_top[:], start=True,
                                 stop=True).then_inc(top_spread, 1)

            def spread(ph):
                n = ph.p
                pe.wait_ge(factors_made, n + 1)
                pe.wait_ge(wh_kept, 16 * n + 16)
                nc.tensor.transpose(ps_w[0:T, 0:P], beta_c[:], ident_f[:]).then_inc(beta_turned, 1)
                pe.wait_ge(hmean_made, n + 1)
                for k in range(K2):
                    ins = nc.tensor.matmul(ps_h[:, 0, 0:F], hmean_b[:, k, :], wcat[:, ph.layer, k, 0:F],
                                           start=(k == 0), stop=(k == K2 - 1))
                ins.then_inc(mean_done, 1)

            def attend(ph, c, q, i):
                k = STEPS * ph.p + NQ * c + q
                kt = 2 * q + i
                if i == 0:
                    pe.wait_ge(g_lo_made, k + 1)
                    if c == 0:
                        pe.wait_ge(v_lo_made, 16 * ph.p + kt + 2)
                for t in range(TC):
                    if kt == 0:
                        wait(pe, acc_kept, 4 * (NC * ph.p + c) + t - 3)
                    hi = g_hi[:, q % 2, i, P * t:P * t + P]
                    lo = g_lo[:, q % 2, i, P * t:P * t + P]
                    nc.tensor.matmul(acc[t][:, 0:FW], hi, v_hi[:, kt, :], start=(kt == 0), stop=False)
                    nc.tensor.matmul(acc[t][:, 0:FW], hi, v_lo[:, kt, :], start=False, stop=False)
                    ins = nc.tensor.matmul(acc[t][:, 0:FW], lo, v_hi[:, kt, :], start=False, stop=(kt == T - 1))
                    if kt == T - 1 and t < TC - 1:
                        ins.then_inc(acc_done, 1)
                if i == 1:
                    ins.then_inc(step_done, 1)

            def phase(ph):
                for s in range(STEPS):
                    c, q = s // NQ, s % NQ
                    for i in range(2):
                        attend(ph, c, q, i)
                        for graph, t in adj_jobs(ph, s):
                            adj_turn(graph, t, i)
                        if ph.next is not None and s in TILE_AT:
                            if i == 0:
                                tile_turn(ph.next.p, TILE_AT[s])
                            else:
                                tile_project(ph.next, TILE_AT[s])
                    if ph.next is not None:
                        if s == REDUCE_AT:
                            maximum_turn(ph.next.p)
                        if s == FACTOR_AT:
                            maximum_spread(ph.next.p)
                        if s == EXP_AT:
                            spread(ph.next)

            pe.wait_ge(consts_made, 3)
            pe.wait_ge(wcat_made, 8)
            pe.wait_ge(vconst_made, 1)
            first = opening()[0]
            for t in range(T):
                tile_turn(0, t)
                tile_project(first, t)
                if t < T // 2:
                    adj_turn(0, t, 0)
                    adj_turn(0, t, 1)
            maximum_turn(0)
            maximum_spread(0)
            spread(first)
            program(pe, phase)


_INS = ["x", "adj", "L0_gnn_W", "L0_gnn_a", "L1_gnn_W", "L1_gnn_a"]


def kernel(**inputs):
    import numpy as np
    import concourse.bacc as bacc
    from concourse.bass_utils import run_bass_kernel_spmd

    nc = bacc.Bacc("TRN2", target_bir_lowering=False, num_devices=1)
    arrays, args = {}, []
    for name in _INS:
        a = np.ascontiguousarray(inputs[name])
        if name.endswith("_a"):
            a = a.reshape(-1)
        arrays[f"in_{name}"] = a
        args.append(nc.dram_tensor(f"in_{name}", a.shape, mybir.dt.from_np(a.dtype), kind="ExternalInput").ap())
    shape = arrays["in_x"].shape
    args.append(nc.dram_tensor("out_x", shape, F32, kind="ExternalOutput").ap())
    gat_kernel(nc, *args)
    r = run_bass_kernel_spmd(nc, [arrays], core_ids=[0])
    return r.results[0]["out_x"]
```

```python
from contextlib import ExitStack

import concourse.bass as bass
from concourse import mybir
from concourse.alu_op_type import AluOpType as ALU


F32 = mybir.dt.float32
F32R = mybir.dt.float32r
BF16 = mybir.dt.bfloat16
U8 = mybir.dt.uint8
ACT = mybir.ActivationFunctionType
AX = mybir.AxisListType.X

P = 128
SLOPE = 0.2
EPS = 1e-5
FLOOR = -80.0


class Phase:

    def __init__(self, p, odd, layer, graph, parity):
        self.p, self.odd, self.layer, self.graph, self.parity = p, odd, layer, graph, parity
        self.prev = self.next = None
        self.late_adj = None
        self.early_adj = None


def gat_kernel(nc, x, adj, w_l0, a_l0, w_l1, a_l1, out):
    B, N, F = x.shape
    T = N // P
    CH = 512
    NC = N // CH
    TC = CH // P
    NQ = T // 2
    STEPS = NC * NQ
    COLS = NC * T
    K2 = F // P
    FW = F + 2
    FV = F + 1
    XS = 4
    GS = 4
    NS = 2

    TILE_AT = {1 + (9 * t) // 8: t for t in range(T)}
    STEP_OF = {t: s for s, t in TILE_AT.items()}
    REDUCE_AT = STEP_OF[T - 1] + 3
    FACTOR_AT = REDUCE_AT + 1
    EXP_AT = FACTOR_AT + 2
    SPREAD_AT = EXP_AT + 1
    HIGH_AT = STEPS - NQ + 1
    REST_AT = HIGH_AT + 2

    assert 3 * NQ <= SPREAD_AT < STEPS and EXP_AT < HIGH_AT

    scratch = nc.dram_tensor("beta_rows", (T, P), F32).ap()
    adj_rows = adj.rearrange("b (t p) j -> b t p j", p=P)
    x_rows = x.rearrange("b (t p) f -> b p t f", p=P)
    out_rows = out.rearrange("b (t p) f -> b p t f", p=P)

    ctx = ExitStack()
    with ctx:
        def sb(name, shape, dt=F32):
            return ctx.enter_context(nc.sbuf_tensor(name, shape, dt))

        def pb(name, shape, dt=F32):
            return ctx.enter_context(nc.psum_tensor(name, shape, dt))

        def sem(name):
            return ctx.enter_context(nc.semaphore(name))

        adj_t = sb("adj_t", [P, 2, T, N], U8)
        adj_in = sb("adj_in", [P, NS, N], BF16)
        xres = sb("xres", [P, 2, T, F])
        x_in = sb("x_in", [P, XS, F])
        hrow = sb("hrow", [P, 2, F])
        hcol = sb("hcol", [P, K2, P])
        wh = sb("wh", [P, T, FW])
        v_hi = sb("v_hi", [P, T, FW], F32R)
        v_lo = sb("v_lo", [P, T, FW], F32R)
        beta_b = sb("beta_b", [P, N])
        g_full = sb("g_full", [P, GS, CH])
        g_hi = sb("g_hi", [P, GS, CH], F32R)
        g_lo = sb("g_lo", [P, GS, CH], F32R)
        wcat = sb("wcat", [P, 2, K2, FW])
        ident_f = sb("ident_f", [P, P])
        ident_b = sb("ident_b", [P, P], BF16)
        ones = sb("ones", [P, P])
        hmean_b = sb("hmean_b", [P, K2, P])
        wh_mean = sb("wh_mean", [P, 2, FV])
        acc_sb = sb("acc_sb", [P, TC, FW])
        expy = sb("expy", [P, 2, F])
        beta_r = sb("beta_r", [T, P])
        stat = sb("stat", [P, 8, 6])
        moment = sb("moment", [P, 8, 2])
        vareps = sb("vareps", [P, 8])
        rstd = sb("rstd", [P, 8])
        shift = sb("shift", [P, 8])
        scaled = sb("scaled", [P, 8])
        minus_half = sb("minus_half", [P, 1])
        eps = sb("eps", [P, 1])
        zero = sb("zero", [P, 1])
        hsum = sb("hsum", [P, K2, T])
        htot = sb("htot", [P, K2])
        fmax = sb("fmax", [P, 1])
        fmax_top = sb("fmax_top", [1, 1])
        fmax_all = sb("fmax_all", [P, 1])
        f2_rel = sb("f2_rel", [P, T])
        f1_top = sb("f1_top", [P, T])
        r_col = sb("r_col", [P, 2, T])
        v_col = sb("v_col", [P, T])
        beta_c = sb("beta_c", [P, T])
        alone = sb("alone", [P, TC])
        rden = sb("rden", [P, TC])

        acc = [pb(f"acc{t}", [P, 512]) for t in range(TC)]
        ps_h = pb("ps_h", [P, K2, P + P])
        ps_w = pb("ps_w", [P, 512])
        ps_a = [pb(f"ps_a{h}", [P, NQ, P], BF16) for h in range(2)]

        setup_dma = sem("setup_dma")
        consts_made = sem("consts_made")
        wcat_made = sem("wcat_made")
        vconst_made = sem("vconst_made")
        x_loaded = [sem(f"x_loaded{i}") for i in range(XS)]
        adj_loaded = [sem(f"adj_loaded{i}") for i in range(NS)]
        res_loaded = [sem(f"res_loaded{c}") for c in range(NC)]
        out_stored = [sem(f"out_stored{c}") for c in range(NC)]
        adj_turned = sem("adj_turned")
        adj_kept = sem("adj_kept")
        stats_made = sem("stats_made")
        moments_made = sem("moments_made")
        rstd_steps = sem("rstd_steps")
        h_made = sem("h_made")
        h_turned = sem("h_turned")
        hcol_made = sem("hcol_made")
        wh_done = sem("wh_done")
        wh_kept = sem("wh_kept")
        reduced = sem("reduced")
        fmax_turned = sem("fmax_turned")
        top_made = sem("top_made")
        top_spread = sem("top_spread")
        fmax_made = sem("fmax_made")
        args_made = sem("args_made")
        one_made = sem("one_made")
        factors_made = sem("factors_made")
        hmean_made = sem("hmean_made")
        beta_turned = sem("beta_turned")
        mean_done = sem("mean_done")
        beta_kept = sem("beta_kept")
        mean_kept = sem("mean_kept")
        beta_stored = sem("beta_stored")
        beta_in_012 = sem("beta_in_012")
        beta_in_3 = sem("beta_in_3")
        v_hi_made = sem("v_hi_made")
        v_lo_made = sem("v_lo_made")
        g_made = sem("g_made")
        g_hi_made = sem("g_hi_made")
        g_lo_made = sem("g_lo_made")
        col_done = sem("col_done")
        acc_done = sem("acc_done")
        acc_kept = sem("acc_kept")
        fix_steps = sem("fix_steps")
        x1_made = sem("x1_made")
        elu_parts = sem("elu_parts")
        elu_half = sem("elu_half")
        out_made = sem("out_made")

        block = ctx.enter_context(nc.Block())

        def wait(eng, semaphore, value):
            if isinstance(value, int) and value <= 0:
                return
            eng.wait_ge(semaphore, value)

        def make(p, odd, layer, graph):
            return Phase(p, odd, layer, graph, graph % 2)

        def opening():
            a, b, c = make(0, 0, 0, 0), make(1, 1, 0, 1), make(2, 0, 1, 0)
            a.next, b.prev, b.next, c.prev = b, a, c, b
            a.early_adj, a.late_adj = 0, 1
            b.early_adj = 1
            return [a, b]

        def middle(r):
            a, b = make(2 * r, 0, 1, r - 1), make(2 * r + 1, 1, 0, r + 1)
            a.prev, a.next, b.prev = make(2 * r - 1, 1, 0, r), b, a
            b.next = make(2 * r + 2, 0, 1, r)
            a.late_adj, b.early_adj = r + 1, r + 1
            return [a, b]

        def closing():
            a, b = make(2 * B - 2, 0, 1, B - 2), make(2 * B - 1, 1, 1, B - 1)
            a.prev, a.next, b.prev = make(2 * B - 3, 1, 0, B - 1), b, a
            return [a, b]

        def program(eng, phase):
            for ph in opening():
                phase(ph)
            with eng.Fori(1, B - 1) as r:
                for ph in middle(r):
                    phase(ph)
            for ph in closing():
                phase(ph)

        def adj_jobs(ph, s):
            if ph.early_adj is not None and s < 16 and s % 2 == 0:
                return [(ph.early_adj, T // 2 + s // 2)]
            if ph.late_adj is not None and s >= 16 and s % 2 == 0:
                return [(ph.late_adj, (s - 16) // 2)]
            return []

        def before(ph, c):
            return (ph, c - 1) if c else (ph.prev, NC - 1)

        @block.sync
        def _(sp):
            for n, (w, a) in enumerate(((w_l0, a_l0), (w_l1, a_l1))):
                with nc.allow_non_contiguous_dma(reason="rows of W and both halves of a for all partitions"):
                    sp.dma_start(wcat[:, n, :, 0:F], w.rearrange("(k p) o -> p k o", p=P)).then_inc(setup_dma, 16)
                    sp.dma_start(g_full[:, n, :], a.partition_broadcast(P)).then_inc(setup_dma, 16)

            def x_tile(n, graph, t):
                j = 16 * n + t
                wait(sp, h_made, j - XS + 1)
                sp.dma_start(x_in[:, t % XS, :], x_rows[graph, :, t, :]).then_inc(x_loaded[t % XS], 16)

            def residual(graph, parity, c):
                if not (isinstance(graph, int) and graph < 2):
                    sp.wait_ge(out_stored[c], 16 * (graph - 1))
                    sp.wait_ge(out_made, 16 * (graph - 2) + 4 * c + 4)
                sp.dma_start(xres[:, parity, TC * c:TC * c + TC, :],
                             x_rows[graph, :, TC * c:TC * c + TC, :]).then_inc(res_loaded[c], 16)

            def store(graph, parity, c):
                sp.wait_ge(out_made, 16 * graph + 4 * c + 4)
                sp.dma_start(out_rows[graph, :, TC * c:TC * c + TC, :],
                             xres[:, parity, TC * c:TC * c + TC, :]).then_inc(out_stored[c], 16)

            def beta(n):
                sp.wait_ge(beta_kept, n + 1)
                sp.dma_start(scratch, beta_r[:, :]).then_inc(beta_stored, 16)
                sp.wait_ge(beta_stored, 16 * (n + 1))
                lot = 3 * TC
                sp.dma_start(beta_b[:, 0:lot * P],
                             scratch[0:lot, :].rearrange("t p -> (t p)").partition_broadcast(P)).then_inc(beta_in_012, 16)

            def beta_rest(n):
                wait(sp, g_made, COLS * n)
                lot = 3 * TC
                sp.dma_start(beta_b[:, lot * P:N],
                             scratch[lot:T, :].rearrange("t p -> (t p)").partition_broadcast(P)).then_inc(beta_in_3, 16)

            def phase(ph):
                nxt = ph.next
                if ph.layer == 0:
                    for c in range(NC - 1):
                        residual(ph.graph, ph.parity, c)
                if ph.prev is not None and ph.prev.layer == 1:
                    store(ph.prev.graph, ph.prev.parity, NC - 1)
                if ph.layer == 0:
                    residual(ph.graph, ph.parity, NC - 1)
                if nxt is not None and nxt.layer == 0:
                    for t in range(T):
                        x_tile(nxt.p, nxt.graph, t)
                if ph.layer == 1:
                    store(ph.graph, ph.parity, 0)
                if nxt is not None:
                    beta(nxt.p)
                if ph.layer == 1:
                    store(ph.graph, ph.parity, 1)
                    if nxt is None:
                        store(ph.graph, ph.parity, 2)
                if nxt is not None:
                    beta_rest(nxt.p)
                if ph.layer == 1 and nxt is not None:
                    store(ph.graph, ph.parity, 2)

            for t in range(T):
                x_tile(0, 0, t)
            beta(0)
            beta_rest(0)
            program(sp, phase)
            store(B - 1, (B - 1) % 2, NC - 1)
            for c in range(NC):
                sp.wait_ge(out_stored[c], 16 * B)

        @block.gpsimd
        def _(pool):
            def adj_load(graph, t):
                j = 16 * graph + t
                wait(pool, adj_turned, 2 * (j - NS) + 2)
                pool.dma_start(adj_in[:, t % NS, :], adj_rows[graph, t, :, :]).then_inc(adj_loaded[t % NS], 16)

            adj_load(0, 0)
            adj_load(0, 1)
            nc.gpsimd.memset(ones[:], 1.0)
            nc.gpsimd.memset(minus_half[:], -0.5)
            nc.gpsimd.memset(eps[:], EPS)
            nc.gpsimd.memset(zero[:], 0.0)
            nc.gpsimd.memset(ident_f[:], 0.0).then_inc(consts_made, 1)
            pool.wait_ge(consts_made, 1)
            nc.gpsimd.affine_select(out=ident_f[:], in_=ident_f[:], compare_op=ALU.not_equal, fill=1.0, base=0,
                                    pattern=[[-1, P]], channel_multiplier=1).then_inc(consts_made, 1)
            pool.wait_ge(consts_made, 2)
            nc.gpsimd.tensor_copy(ident_b[:], ident_f[:]).then_inc(consts_made, 1)
            pool.wait_ge(consts_made, 3)

            def tile_rstd(n, t):
                j, q = 16 * n + t, t % 8
                pool.wait_ge(moments_made, j + 1)
                wait(pool, h_made, j - 7)
                col = slice(q, q + 1)
                nc.gpsimd.tensor_tensor(vareps[:, col], moment[:, q, 1:2], eps[:], ALU.add).then_inc(rstd_steps, 1)
                pool.wait_ge(rstd_steps, 4 * j + 1)
                nc.gpsimd.tensor_tensor(rstd[:, col], vareps[:, col], minus_half[:], ALU.pow).then_inc(rstd_steps, 1)
                pool.wait_ge(rstd_steps, 4 * j + 2)
                nc.gpsimd.tensor_tensor(scaled[:, col], moment[:, q, 0:1], rstd[:, col],
                                        ALU.mult).then_inc(rstd_steps, 1)
                pool.wait_ge(rstd_steps, 4 * j + 3)
                nc.gpsimd.tensor_tensor(shift[:, col], zero[:], scaled[:, col], ALU.subtract).then_inc(rstd_steps, 1)

            def phase(ph):
                for s in range(STEPS):
                    for graph, t in adj_jobs(ph, s):
                        adj_load(graph, t)
                    if ph.next is not None and s in TILE_AT:
                        tile_rstd(ph.next.p, TILE_AT[s])

            for t in range(T):
                tile_rstd(0, t)
                if NS <= t + NS < T // 2:
                    adj_load(0, t + NS)
            program(pool, phase)

        @block.vector
        def _(dve):
            def edge_weights(ph, c, kt):
                k = COLS * ph.p + T * c + kt
                if kt == 0:
                    dve.wait_ge(adj_kept, 32 * ph.graph + 8 * c + 8)
                    dve.wait_ge(beta_in_012 if c < NC - 1 else beta_in_3, 16 * (ph.p + 1))
                    dve.wait_ge(factors_made, ph.p + 1)
                wait(dve, g_lo_made, k - GS + 1)
                nc.vector.scalar_tensor_tensor(
                    out=g_full[:, kt % GS, :], in0=beta_b[:, CH * c:CH * c + CH],
                    scalar=r_col[:, ph.odd, kt:kt + 1], in1=adj_t[:, ph.parity, kt, CH * c:CH * c + CH],
                    op0=ALU.max, op1=ALU.mult).then_inc(g_made, 1)

            def edge_weights_ahead(ph, s, i):
                if s + 1 < STEPS:
                    edge_weights(ph, (s + 1) // NQ, 2 * ((s + 1) % NQ) + i)
                elif ph.next is not None:
                    edge_weights(ph.next, 0, i)

            def edge_rest(ph, c, kt):
                k = COLS * ph.p + T * c + kt
                dve.wait_ge(g_hi_made, k + 1)
                wait(dve, col_done, k - GS + 1)
                nc.vector.tensor_tensor(g_lo[:, kt % GS, :], g_full[:, kt % GS, :],
                                        g_hi[:, kt % GS, :].bitcast(F32), ALU.subtract).then_inc(g_lo_made, 1)

            def rows_ready(ph, t):
                if ph.layer == 0:
                    dve.wait_ge(x_loaded[t % XS], 16 * (T // XS * ph.graph + t // XS + 1))
                else:
                    dve.wait_ge(x1_made, 16 * ph.graph + t + 1)
                wait(dve, rstd_steps, 4 * (16 * ph.p + t - 7))

            def tile_stats(ph, t):
                src = x_in[:, t % XS, :] if ph.layer == 0 else xres[:, ph.parity, t, :]
                nc.vector.bn_stats(stat[:, t % 8, :], src).then_inc(stats_made, 1)

            def stats_ready(ph, t):
                dve.wait_ge(stats_made, 16 * ph.p + t + 1)

            def tile_moments(t):
                nc.vector.bn_aggr(moment[:, t % 8, :], stat[:, t % 8, :]).then_inc(moments_made, 1)

            def reduce(n):
                dve.wait_ge(wh_kept, 16 * n + 16)
                nc.vector.tensor_reduce(out=htot[:], in_=hsum[:, :, :], axis=AX, op=ALU.add).then_inc(reduced, 1)
                nc.vector.tensor_reduce(out=fmax[:], in_=wh[:, :, F + 1], axis=AX, op=ALU.max).then_inc(reduced, 1)

            def top(n):
                dve.wait_ge(fmax_turned, n + 1)
                nc.vector.tensor_reduce(out=fmax_top[:], in_=ps_w[0:1, 0:P], axis=AX, op=ALU.max).then_inc(top_made, 1)

            def arguments(n):
                dve.wait_ge(top_spread, n + 1)
                nc.vector.tensor_copy(fmax_all[:], ps_w[:, P:P + 1]).then_inc(fmax_made, 1)
                dve.wait_ge(fmax_made, n + 1)
                nc.vector.tensor_scalar(f2_rel[:], wh[:, :, F + 1], fmax_all[:], FLOOR,
                                        ALU.subtract, ALU.max).then_inc(args_made, 1)
                nc.vector.tensor_scalar(f1_top[:], wh[:, :, F], fmax_all[:], 0.0,
                                        ALU.add, ALU.max).then_inc(args_made, 1)
                dve.wait_ge(args_made, 2 * n + 2)
                nc.vector.memset(wh[:, :, F:F + 1], 1.0).then_inc(one_made, 1)

            def values_rest(n, m):
                for kt in (2 * m, 2 * m + 1):
                    dve.wait_ge(v_hi_made, 16 * n + kt + 1)
                    nc.vector.scalar_tensor_tensor(
                        out=v_lo[:, kt, 0:FV], in0=wh[:, kt, 0:FV], scalar=v_col[:, kt:kt + 1],
                        in1=v_hi[:, kt, 0:FV].bitcast(F32), op0=ALU.mult, op1=ALU.subtract).then_inc(v_lo_made, 1)

            def chunk_end(ph, c, q):
                k = NC * ph.p + c
                if q == 1:
                    dve.wait_ge(acc_kept, 4 * k + 4)
                    nc.vector.tensor_scalar(alone[:], acc_sb[:, :, F + 1], 0.0, None,
                                            ALU.is_equal).then_inc(fix_steps, 1)
                if q in (2, 3):
                    if q == 2:
                        dve.wait_ge(fix_steps, 6 * k + 1)
                        dve.wait_ge(mean_kept, ph.p + 1)
                    for t in (2 * q - 4, 2 * q - 3):
                        nc.vector.scalar_tensor_tensor(
                            out=acc_sb[:, t, 0:FV], in0=wh_mean[:, ph.odd, :], scalar=alone[:, t:t + 1],
                            in1=acc_sb[:, t, 0:FV], op0=ALU.mult, op1=ALU.add).then_inc(fix_steps, 1)
                if q == 3:
                    dve.wait_ge(fix_steps, 6 * k + 5)
                    nc.vector.reciprocal(rden[:], acc_sb[:, :, F]).then_inc(fix_steps, 1)
                if q in (4, 5) and ph.layer == 0:
                    if q == 4:
                        dve.wait_ge(fix_steps, 6 * k + 6)
                        dve.wait_ge(res_loaded[c], 16 * (ph.graph + 1))
                    for t in (2 * q - 8, 2 * q - 7):
                        row = xres[:, ph.parity, TC * c + t, :]
                        nc.vector.scalar_tensor_tensor(out=row, in0=acc_sb[:, t, 0:F], scalar=rden[:, t:t + 1],
                                                       in1=row, op0=ALU.mult, op1=ALU.add).then_inc(x1_made, 1)
                if q in (5, 7) and ph.layer == 1:
                    lot = (q - 5, q - 4)
                    j = 16 * ph.graph + 4 * c
                    for t in lot:
                        dve.wait_ge(elu_parts, j + t + 1)
                        e = expy[:, t % 2, :]
                        nc.vector.scalar_tensor_tensor(out=e, in0=e, scalar=1.0, in1=acc_sb[:, t, 0:F],
                                                       op0=ALU.min, op1=ALU.add).then_inc(elu_half, 1)
                    for t in lot:
                        dve.wait_ge(elu_half, j + t + 1)
                        row = xres[:, ph.parity, TC * c + t, :]
                        nc.vector.scalar_tensor_tensor(out=row, in0=expy[:, t % 2, :], scalar=-1.0, in1=row,
                                                       op0=ALU.add, op1=ALU.add).then_inc(out_made, 1)

            def phase(ph):
                for s in range(STEPS):
                    c, q = s // NQ, s % NQ
                    has_tile = ph.next is not None and s + 1 in TILE_AT
                    if has_tile:
                        rows_ready(ph.next, TILE_AT[s + 1])
                    edge_weights_ahead(ph, s, 0)
                    if has_tile:
                        tile_stats(ph.next, TILE_AT[s + 1])
                    edge_rest(ph, c, 2 * q)
                    if has_tile:
                        stats_ready(ph.next, TILE_AT[s + 1])
                    edge_weights_ahead(ph, s, 1)
                    edge_rest(ph, c, 2 * q + 1)
                    if has_tile:
                        tile_moments(TILE_AT[s + 1])
                    late, at = before(ph, c)
                    if late is not None:
                        chunk_end(late, at, q)
                    if s < REST_AT + NQ - STEPS and ph.prev is not None:
                        values_rest(ph.p, STEPS - REST_AT + s)
                    if ph.next is not None:
                        if s == REDUCE_AT:
                            reduce(ph.next.p)
                        if s == FACTOR_AT:
                            top(ph.next.p)
                        if s == FACTOR_AT + 1:
                            arguments(ph.next.p)
                        if s >= REST_AT:
                            values_rest(ph.next.p, s - REST_AT)

            dve.wait_ge(setup_dma, 64)
            for n in range(2):
                for k in range(K2):
                    for i in range(2):
                        ins = nc.vector.tensor_tensor_reduce(
                            out=g_full[:, 2 + n, F * i:F * i + F], in0=wcat[:, n, k, 0:F],
                            in1=g_full[:, n, F * i:F * i + F], scale=1.0, scalar=0.0, op0=ALU.mult, op1=ALU.add,
                            accum_out=wcat[:, n, k, F + i:F + i + 1])
                        ins.then_inc(wcat_made, 1)
                        dve.wait_ge(wcat_made, 4 * n + 2 * k + i + 1)
            nc.vector.memset(v_hi[:, :, F + 1:F + 2].bitcast(F32), 1.0)
            nc.vector.memset(v_lo[:, :, F + 1:F + 2].bitcast(F32), 0.0)
            nc.vector.memset(wh_mean[:, :, F:F + 1], 1.0).then_inc(vconst_made, 1)
            dve.wait_ge(vconst_made, 1)
            first = opening()[0]
            for t in range(T):
                rows_ready(first, t)
                tile_stats(first, t)
                stats_ready(first, t)
                tile_moments(t)
            reduce(0)
            top(0)
            arguments(0)
            for m in range(NQ):
                values_rest(0, m)
            for i in range(2):
                edge_weights(first, 0, i)
            program(dve, phase)
            last = closing()[1]
            for q in range(NQ):
                chunk_end(last, NC - 1, q)

        @block.scalar
        def _(act):
            def adj_keep(graph, t):
                j = 16 * graph + t
                for h in range(2):
                    act.wait_ge(adj_turned, 2 * j + h + 1)
                    nc.scalar.activation(adj_t[:, graph % 2, NQ * h:NQ * h + NQ, P * t:P * t + P], ps_a[h][:, :, :],
                                         ACT.Copy).then_inc(adj_kept, 1)

            def tile_normalise(ph, t):
                j, q = 16 * ph.p + t, t % 8
                act.wait_ge(rstd_steps, 4 * j + 4)
                wait(act, h_turned, j - 1)
                src = x_in[:, t % XS, :] if ph.layer == 0 else xres[:, ph.parity, t, :]
                nc.scalar.activation(hrow[:, t % 2, :], src, ACT.Relu, bias=shift[:, q:q + 1],
                                     scale=rstd[:, q:q + 1]).then_inc(h_made, 1)

            def tile_columns(ph, t):
                j = 16 * ph.p + t
                act.wait_ge(h_turned, j + 1)
                wait(act, wh_done, j)
                if t == 0:
                    wait(act, reduced, 2 * ph.p)
                for k in range(K2):
                    ins = nc.scalar.activation(hcol[:, k, :], ps_h[:, k, 0:P], ACT.Copy,
                                               accum_out=hsum[:, k, t:t + 1])
                ins.then_inc(hcol_made, 1)

            def tile_keep(ph, t):
                j = 16 * ph.p + t
                act.wait_ge(wh_done, j + 1)
                wait(act, v_lo_made, j - 15)
                nc.scalar.activation(wh[:, t, :], ps_w[:, 0:FW], ACT.Copy).then_inc(wh_kept, 1)

            def factors(ph):
                n = ph.p
                act.wait_ge(args_made, 2 * n + 2)
                nc.scalar.activation(r_col[:, ph.odd, :], f2_rel[:], ACT.Exp, scale=1.0 - SLOPE)
                nc.scalar.activation(v_col[:], f2_rel[:], ACT.Exp, scale=SLOPE)
                nc.scalar.activation(beta_c[:], f1_top[:], ACT.Exp, scale=SLOPE - 1.0).then_inc(factors_made, 1)
                act.wait_ge(reduced, 2 * n + 2)
                for k in range(K2):
                    ins = nc.scalar.activation(hmean_b[:, k, :], ones[:], ACT.Copy, scale=htot[:, k:k + 1])
                ins.then_inc(hmean_made, 1)

            def spread(ph):
                n = ph.p
                act.wait_ge(beta_turned, n + 1)
                wait(act, beta_stored, 16 * n)
                nc.scalar.activation(beta_r[:], ps_w[0:T, 0:P], ACT.Copy).then_inc(beta_kept, 1)
                act.wait_ge(mean_done, n + 1)
                nc.scalar.activation(wh_mean[:, ph.odd, 0:F], ps_h[:, 0, 0:F], ACT.Copy,
                                     scale=1.0 / N).then_inc(mean_kept, 1)

            def values_high(n, m):
                act.wait_ge(one_made, n + 1)
                act.wait_ge(factors_made, n + 1)
                wait(act, col_done, COLS * (n - 1) + 3 * T + 2 * m + 2)
                for kt in (2 * m, 2 * m + 1):
                    nc.scalar.activation(v_hi[:, kt, 0:FV], wh[:, kt, 0:FV], ACT.Copy,
                                         scale=v_col[:, kt:kt + 1]).then_inc(v_hi_made, 1)

            def edge_high(ph, c, kt):
                k = COLS * ph.p + T * c + kt
                act.wait_ge(g_made, k + 1)
                wait(act, col_done, k - GS + 1)
                nc.scalar.activation(g_hi[:, kt % GS, :], g_full[:, kt % GS, :], ACT.Copy).then_inc(g_hi_made, 1)

            def edge_high_ahead(ph, s, i):
                if s + 1 < STEPS:
                    edge_high(ph, (s + 1) // NQ, 2 * ((s + 1) % NQ) + i)
                elif ph.next is not None:
                    edge_high(ph.next, 0, i)

            def acc_keep(ph, c):
                k = NC * ph.p + c
                late, at = before(ph, c)
                if late is not None:
                    act.wait_ge(out_made if late.layer else x1_made, 16 * late.graph + 4 * at + 4)
                for t in range(TC):
                    if t < TC - 1:
                        act.wait_ge(acc_done, 3 * k + t + 1)
                    else:
                        act.wait_ge(col_done, T * (k + 1))
                    nc.scalar.activation(acc_sb[:, t, :], acc[t][:, 0:FW], ACT.Copy).then_inc(acc_kept, 1)

            def elu(ph, c, q):
                k = NC * ph.p + c
                j = 16 * ph.graph + 4 * c
                act.wait_ge(fix_steps, 6 * k + 6)
                for t in (q - 3, q - 2):
                    if t >= 2:
                        act.wait_ge(out_made, j + t - 1)
                    nc.scalar.activation(expy[:, t % 2, :], acc_sb[:, t, 0:F], ACT.Exp, scale=rden[:, t:t + 1])
                    nc.scalar.activation(acc_sb[:, t, 0:F], acc_sb[:, t, 0:F], ACT.Relu,
                                         scale=rden[:, t:t + 1]).then_inc(elu_parts, 1)

            def phase(ph):
                for s in range(STEPS):
                    c, q = s // NQ, s % NQ
                    late, at = before(ph, c)
                    if q == 0 and late is not None:
                        acc_keep(late, at)
                    edge_high_ahead(ph, s, 0)
                    if ph.next is not None:
                        if s - 3 in TILE_AT:
                            tile_keep(ph.next, TILE_AT[s - 3])
                        if s - 2 in TILE_AT:
                            tile_columns(ph.next, TILE_AT[s - 2])
                    edge_high_ahead(ph, s, 1)
                    if ph.next is not None and s in TILE_AT:
                        tile_normalise(ph.next, TILE_AT[s])
                    if late is not None and late.layer == 1 and q in (3, 5):
                        elu(late, at, q)
                    for graph, t in adj_jobs(ph, s):
                        adj_keep(graph, t)
                    if s < HIGH_AT + NQ - STEPS and ph.prev is not None:
                        values_high(ph.p, STEPS - HIGH_AT + s)
                    if ph.next is not None:
                        if s == EXP_AT:
                            factors(ph.next)
                        if s == SPREAD_AT:
                            spread(ph.next)
                        if s >= HIGH_AT:
                            values_high(ph.next.p, s - HIGH_AT)

            first = opening()[0]
            for t in range(T):
                tile_normalise(first, t)
                tile_columns(first, t)
                tile_keep(first, t)
                if t < T // 2:
                    adj_keep(0, t)
            factors(first)
            spread(first)
            for m in range(NQ):
                values_high(0, m)
            for i in range(2):
                edge_high(first, 0, i)
            program(act, phase)
            last = closing()[1]
            acc_keep(last, NC - 1)
            for q in (3, 5):
                elu(last, NC - 1, q)

        @block.tensor
        def _(pe):
            def adj_turn(graph, t, h):
                j = 16 * graph + t
                if h == 0:
                    pe.wait_ge(adj_loaded[t % NS], 16 * (8 * graph + t // 2 + 1))
                wait(pe, adj_kept, 2 * j + h - 1)
                for i in range(NQ):
                    kt = NQ * h + i
                    ins = nc.tensor.transpose(ps_a[h][:, i, :], adj_in[:, t % NS, P * kt:P * kt + P], ident_b[:])
                ins.then_inc(adj_turned, 1)

            def tile_turn(n, t):
                j = 16 * n + t
                pe.wait_ge(h_made, j + 1)
                wait(pe, hcol_made, j)
                if t == 0:
                    wait(pe, mean_kept, n)
                for k in range(K2):
                    ins = nc.tensor.transpose(ps_h[:, k, 0:P], hrow[:, t % 2, P * k:P * k + P], ident_f[:])
                ins.then_inc(h_turned, 1)

            def tile_project(ph, t):
                n = ph.p
                j = 16 * n + t
                pe.wait_ge(hcol_made, j + 1)
                wait(pe, wh_kept, j)
                if t == 0:
                    wait(pe, beta_kept, n)
                for k in range(K2):
                    ins = nc.tensor.matmul(ps_w[:, 0:FW], hcol[:, k, :], wcat[:, ph.layer, k, :],
                                           start=(k == 0), stop=(k == K2 - 1))
                ins.then_inc(wh_done, 1)

            def maximum_turn(n):
                pe.wait_ge(reduced, 2 * n + 2)
                nc.tensor.transpose(ps_w[0:1, 0:P], fmax[:], ident_f[:]).then_inc(fmax_turned, 1)

            def maximum_spread(n):
                pe.wait_ge(top_made, n + 1)
                nc.tensor.matmul(ps_w[:, P:P + 1], ones[0:1, :], fmax_top[:], start=True,
                                 stop=True).then_inc(top_spread, 1)

            def spread(ph):
                n = ph.p
                pe.wait_ge(factors_made, n + 1)
                pe.wait_ge(wh_kept, 16 * n + 16)
                nc.tensor.transpose(ps_w[0:T, 0:P], beta_c[:], ident_f[:]).then_inc(beta_turned, 1)
                pe.wait_ge(hmean_made, n + 1)
                for k in range(K2):
                    ins = nc.tensor.matmul(ps_h[:, 0, 0:F], hmean_b[:, k, :], wcat[:, ph.layer, k, 0:F],
                                           start=(k == 0), stop=(k == K2 - 1))
                ins.then_inc(mean_done, 1)

            def attend(ph, c, kt):
                k = COLS * ph.p + T * c + kt
                pe.wait_ge(g_lo_made, k + 1)
                if c == 0:
                    pe.wait_ge(v_lo_made, 16 * ph.p + kt + 1)
                for t in range(TC):
                    if kt == 0:
                        wait(pe, acc_kept, 4 * (NC * ph.p + c) + t - 3)
                    hi = g_hi[:, kt % GS, P * t:P * t + P]
                    lo = g_lo[:, kt % GS, P * t:P * t + P]
                    nc.tensor.matmul(acc[t][:, 0:FW], hi, v_hi[:, kt, :], start=(kt == 0), stop=False)
                    nc.tensor.matmul(acc[t][:, 0:FW], hi, v_lo[:, kt, :], start=False, stop=False)
                    ins = nc.tensor.matmul(acc[t][:, 0:FW], lo, v_hi[:, kt, :], start=False, stop=(kt == T - 1))
                    if kt == T - 1 and t < TC - 1:
                        ins.then_inc(acc_done, 1)
                ins.then_inc(col_done, 1)

            def phase(ph):
                for s in range(STEPS):
                    c, q = s // NQ, s % NQ
                    for i in range(2):
                        attend(ph, c, 2 * q + i)
                        for graph, t in adj_jobs(ph, s):
                            adj_turn(graph, t, i)
                    if ph.next is not None and s - 2 in TILE_AT:
                        tile_project(ph.next, TILE_AT[s - 2])
                    if ph.next is not None and s - 1 in TILE_AT:
                        tile_turn(ph.next.p, TILE_AT[s - 1])
                    if ph.next is not None:
                        if s == REDUCE_AT:
                            maximum_turn(ph.next.p)
                        if s == FACTOR_AT:
                            maximum_spread(ph.next.p)
                        if s == EXP_AT:
                            spread(ph.next)

            pe.wait_ge(consts_made, 3)
            pe.wait_ge(wcat_made, 8)
            pe.wait_ge(vconst_made, 1)
            first = opening()[0]
            for t in range(T):
                tile_turn(0, t)
                tile_project(first, t)
                if t < T // 2:
                    adj_turn(0, t, 0)
                    adj_turn(0, t, 1)
            maximum_turn(0)
            maximum_spread(0)
            spread(first)
            program(pe, phase)


_INS = ["x", "adj", "L0_gnn_W", "L0_gnn_a", "L1_gnn_W", "L1_gnn_a"]


def kernel(**inputs):
    import numpy as np
    import concourse.bacc as bacc
    from concourse.bass_utils import run_bass_kernel_spmd

    nc = bacc.Bacc("TRN2", target_bir_lowering=False, num_devices=1)
    arrays, args = {}, []
    for name in _INS:
        a = np.ascontiguousarray(inputs[name])
        if name.endswith("_a"):
            a = a.reshape(-1)
        arrays[f"in_{name}"] = a
        args.append(nc.dram_tensor(f"in_{name}", a.shape, mybir.dt.from_np(a.dtype), kind="ExternalInput").ap())
    shape = arrays["in_x"].shape
    args.append(nc.dram_tensor("out_x", shape, F32, kind="ExternalOutput").ap())
    gat_kernel(nc, *args)
    r = run_bass_kernel_spmd(nc, [arrays], core_ids=[0])
    return r.results[0]["out_x"]
```

```python
from contextlib import ExitStack

import concourse.bass as bass
from concourse import mybir
from concourse.alu_op_type import AluOpType as ALU


F32 = mybir.dt.float32
F32R = mybir.dt.float32r
BF16 = mybir.dt.bfloat16
U8 = mybir.dt.uint8
U16 = mybir.dt.uint16
ACT = mybir.ActivationFunctionType
AX = mybir.AxisListType.X

P = 128
SLOPE = 0.2
EPS = 1e-5
FLOOR = -80.0


class Phase:

    def __init__(self, p, odd, layer, graph, parity):
        self.p, self.odd, self.layer, self.graph, self.parity = p, odd, layer, graph, parity
        self.prev = self.next = None
        self.late_adj = None
        self.early_adj = None
        self.first = isinstance(p, int) and p == 0


def gat_kernel(nc, x, adj, w_l0, a_l0, w_l1, a_l1, out):
    B, N, F = x.shape
    T = N // P
    CH = 512
    NC = N // CH
    TC = CH // P
    NQ = T // 2
    STEPS = NC * NQ
    COLS = NC * T
    K2 = F // P
    FW = F + 2
    FV = F + 1
    XS = 4
    GS = 2
    NS = 2

    TILE_AT = {1 + (6 * t) // 5: t for t in range(T)}
    REDUCE_AT = max(TILE_AT) + 4
    FACTOR_AT = REDUCE_AT + 1
    EXP_AT = FACTOR_AT + 2
    SPREAD_AT = EXP_AT + 1
    HIGH_AT = STEPS - NQ + 4
    REST_AT = HIGH_AT + 2

    LATE = 9
    LATE_AT = {22 + t: t for t in range(LATE)}
    EARLY_AT = {i: LATE + i for i in range(T - LATE)}
    assert all(s >= NQ * (t // TC + 1) for s, t in LATE_AT.items())
    assert all(s <= 3 * NQ - 2 for s in EARLY_AT)

    assert 3 * NQ <= SPREAD_AT < STEPS and EXP_AT <= HIGH_AT

    scratch = nc.dram_tensor("beta_rows", (T, P), F32).ap()
    adj_rows = adj.rearrange("b (t p) j -> b t p j", p=P)
    x_rows = x.rearrange("b (t p) f -> b p t f", p=P)
    out_rows = out.rearrange("b (t p) f -> b p t f", p=P)

    ctx = ExitStack()
    with ctx:
        def sb(name, shape, dt=F32):
            return ctx.enter_context(nc.sbuf_tensor(name, shape, dt))

        def pb(name, shape, dt=F32):
            return ctx.enter_context(nc.psum_tensor(name, shape, dt))

        def sem(name):
            return ctx.enter_context(nc.semaphore(name))

        adj_t = sb("adj_t", [P, 2, NQ, N], U16)
        adj_in = sb("adj_in", [P, NS, N], BF16)
        xres = sb("xres", [P, 2, T, F])
        x_in = sb("x_in", [P, XS, F])
        hrow = sb("hrow", [P, 2, F])
        hcol = sb("hcol", [P, K2, P])
        wh = sb("wh", [P, T, FW])
        v_hi = sb("v_hi", [P, T, FW], F32R)
        v_lo = sb("v_lo", [P, T, FW], F32R)
        beta_b = sb("beta_b", [P, N])
        g_full = sb("g_full", [P, GS, 2, CH])
        g_hi = sb("g_hi", [P, GS, 2, CH], F32R)
        g_lo = sb("g_lo", [P, GS, 2, CH], F32R)
        wcat = sb("wcat", [P, 2, K2, FW])
        ident_f = sb("ident_f", [P, P])
        ident_b = sb("ident_b", [P, 2, P], BF16)
        ones = sb("ones", [P, P])
        hmean_b = sb("hmean_b", [P, K2, P])
        wh_mean = sb("wh_mean", [P, 2, FV])
        acc_sb = sb("acc_sb", [P, TC, FW])
        expy = sb("expy", [P, 2, F])
        beta_r = sb("beta_r", [T, P])
        stat = sb("stat", [P, 8, 6])
        moment = sb("moment", [P, 8, 2])
        vareps = sb("vareps", [P, 8])
        rstd = sb("rstd", [P, 8])
        shift = sb("shift", [P, 8])
        scaled = sb("scaled", [P, 8])
        minus_half = sb("minus_half", [P, 1])
        eps = sb("eps", [P, 1])
        zero = sb("zero", [P, 1])
        hsum = sb("hsum", [P, K2, T])
        htot = sb("htot", [P, K2])
        fmax = sb("fmax", [P, 1])
        fmax_top = sb("fmax_top", [1, 1])
        fmax_all = sb("fmax_all", [P, 1])
        f2_rel = sb("f2_rel", [P, T])
        f1_top = sb("f1_top", [P, T])
        r_col = sb("r_col", [P, 2, T])
        v_col = sb("v_col", [P, T])
        beta_c = sb("beta_c", [P, T])
        alone = sb("alone", [P, TC], U8)
        rden = sb("rden", [P, TC])

        acc = [pb(f"acc{t}", [P, 512]) for t in range(TC)]
        ps_h = pb("ps_h", [P, K2, P + P])
        ps_w = pb("ps_w", [P, 512])
        ps_a = [pb(f"ps_a{h}", [P, NQ // 2, P]) for h in range(2)]

        lead_h = [acc[t][:, :].rearrange("p (k i) -> p k i", k=K2) for t in range(2)]
        lead_w = [acc[2 + t] for t in range(2)]
        lead_col = [expy[:, i, :].rearrange("p (k i) -> p k i", k=K2) for i in range(2)]

        setup_dma = sem("setup_dma")
        consts_made = sem("consts_made")
        wcat_made = sem("wcat_made")
        vconst_made = sem("vconst_made")
        x_loaded = [sem(f"x_loaded{i}") for i in range(XS)]
        adj_loaded = [sem(f"adj_loaded{i}") for i in range(NS)]
        res_loaded = [sem(f"res_loaded{c}") for c in range(NC)]
        out_stored = [sem(f"out_stored{c}") for c in range(NC)]
        adj_turned = sem("adj_turned")
        adj_kept = sem("adj_kept")
        stats_made = sem("stats_made")
        moments_made = sem("moments_made")
        rstd_steps = sem("rstd_steps")
        h_made = sem("h_made")
        h_turned = sem("h_turned")
        hcol_made = sem("hcol_made")
        wh_done = sem("wh_done")
        wh_kept = sem("wh_kept")
        reduced = sem("reduced")
        fmax_turned = sem("fmax_turned")
        top_made = sem("top_made")
        top_spread = sem("top_spread")
        fmax_made = sem("fmax_made")
        args_made = sem("args_made")
        one_made = sem("one_made")
        factors_made = sem("factors_made")
        hmean_made = sem("hmean_made")
        beta_turned = sem("beta_turned")
        mean_done = sem("mean_done")
        beta_kept = sem("beta_kept")
        mean_kept = sem("mean_kept")
        beta_stored = sem("beta_stored")
        beta_in_012 = sem("beta_in_012")
        beta_in_3 = sem("beta_in_3")
        v_made = sem("v_made")
        v_hi_made = sem("v_hi_made")
        v_lo_made = sem("v_lo_made")
        g_made = sem("g_made")
        g_hi_made = sem("g_hi_made")
        g_lo_made = sem("g_lo_made")
        pair_done = sem("pair_done")
        acc_done = sem("acc_done")
        acc_kept = sem("acc_kept")
        fix_steps = sem("fix_steps")
        x1_made = sem("x1_made")
        elu_parts = sem("elu_parts")
        elu_half = sem("elu_half")
        out_made = sem("out_made")

        block = ctx.enter_context(nc.Block())

        def wait(eng, semaphore, value):
            if isinstance(value, int) and value <= 0:
                return
            eng.wait_ge(semaphore, value)

        def make(p, odd, layer, graph):
            return Phase(p, odd, layer, graph, graph % 2)

        def opening():
            a, b, c = make(0, 0, 0, 0), make(1, 1, 0, 1), make(2, 0, 1, 0)
            a.next, b.prev, b.next, c.prev = b, a, c, b
            a.late_adj = 1
            b.early_adj = 1
            return [a, b]

        def middle(r):
            a, b = make(2 * r, 0, 1, r - 1), make(2 * r + 1, 1, 0, r + 1)
            a.prev, a.next, b.prev = make(2 * r - 1, 1, 0, r), b, a
            b.next = make(2 * r + 2, 0, 1, r)
            a.late_adj, b.early_adj = r + 1, r + 1
            return [a, b]

        def closing():
            a, b = make(2 * B - 2, 0, 1, B - 2), make(2 * B - 1, 1, 1, B - 1)
            a.prev, a.next, b.prev = make(2 * B - 3, 1, 0, B - 1), b, a
            return [a, b]

        def program(eng, phase):
            for ph in opening():
                phase(ph)
            with eng.Fori(1, B - 1) as r:
                for ph in middle(r):
                    phase(ph)
            for ph in closing():
                phase(ph)

        def adj_jobs(ph, s):
            if ph.first and 0 <= s < T - TC:
                return [(0, TC + s)]
            if ph.early_adj is not None and s in EARLY_AT:
                return [(ph.early_adj, EARLY_AT[s])]
            if ph.late_adj is not None and s in LATE_AT:
                return [(ph.late_adj, LATE_AT[s])]
            return []

        def before(ph, c):
            return (ph, c - 1) if c else (ph.prev, NC - 1)

        @block.sync
        def _(sp):
            def weights(n, w, a):
                with nc.allow_non_contiguous_dma(reason="rows of W and both halves of a for all partitions"):
                    sp.dma_start(wcat[:, n, :, 0:F], w.rearrange("(k p) o -> p k o", p=P)).then_inc(setup_dma, 16)
                    sp.dma_start(g_full[:, 0, n, :], a.partition_broadcast(P)).then_inc(setup_dma, 16)

            def x_tile(n, graph, t):
                j = 16 * n + t
                wait(sp, h_made, j - XS + 1)
                sp.dma_start(x_in[:, t % XS, :], x_rows[graph, :, t, :]).then_inc(x_loaded[t % XS], 16)

            def residual(graph, parity, c):
                if not (isinstance(graph, int) and graph < 2):
                    sp.wait_ge(out_stored[c], 16 * (graph - 1))
                    sp.wait_ge(out_made, 16 * (graph - 2) + 4 * c + 4)
                sp.dma_start(xres[:, parity, TC * c:TC * c + TC, :],
                             x_rows[graph, :, TC * c:TC * c + TC, :]).then_inc(res_loaded[c], 16)

            def store(graph, parity, c):
                sp.wait_ge(out_made, 16 * graph + 4 * c + 4)
                sp.dma_start(out_rows[graph, :, TC * c:TC * c + TC, :],
                             xres[:, parity, TC * c:TC * c + TC, :]).then_inc(out_stored[c], 16)

            def beta(n):
                sp.wait_ge(beta_kept, n + 1)
                sp.dma_start(scratch, beta_r[:, :]).then_inc(beta_stored, 16)
                sp.wait_ge(beta_stored, 16 * (n + 1))
                lot = 3 * TC
                sp.dma_start(beta_b[:, 0:lot * P],
                             scratch[0:lot, :].rearrange("t p -> (t p)").partition_broadcast(P)).then_inc(beta_in_012, 16)

            def beta_rest(n):
                wait(sp, g_made, COLS * n)
                lot = 3 * TC
                sp.dma_start(beta_b[:, lot * P:N],
                             scratch[lot:T, :].rearrange("t p -> (t p)").partition_broadcast(P)).then_inc(beta_in_3, 16)

            def phase(ph):
                nxt = ph.next
                if ph.layer == 0:
                    for c in range(NC - 1):
                        residual(ph.graph, ph.parity, c)
                if ph.prev is not None and ph.prev.layer == 1:
                    store(ph.prev.graph, ph.prev.parity, NC - 1)
                if ph.layer == 0:
                    residual(ph.graph, ph.parity, NC - 1)
                if nxt is not None and nxt.layer == 0:
                    for t in range(XS if ph.first else 0, T):
                        x_tile(nxt.p, nxt.graph, t)
                if ph.layer == 1:
                    store(ph.graph, ph.parity, 0)
                if nxt is not None:
                    beta(nxt.p)
                if ph.layer == 1:
                    store(ph.graph, ph.parity, 1)
                    if nxt is None:
                        store(ph.graph, ph.parity, 2)
                if nxt is not None:
                    beta_rest(nxt.p)
                if ph.layer == 1 and nxt is not None:
                    store(ph.graph, ph.parity, 2)

            for t in range(T):
                x_tile(0, 0, t)
                if t == XS - 1:
                    weights(0, w_l0, a_l0)
                    weights(1, w_l1, a_l1)
            for t in range(XS):
                x_tile(1, 1, t)
            beta(0)
            beta_rest(0)
            program(sp, phase)
            store(B - 1, (B - 1) % 2, NC - 1)
            for c in range(NC):
                sp.wait_ge(out_stored[c], 16 * B)

        @block.gpsimd
        def _(pool):
            def adj_load(graph, t):
                j = 16 * graph + t
                wait(pool, adj_turned, 2 * (j - NS) + 2)
                pool.dma_start(adj_in[:, t % NS, :], adj_rows[graph, t, :, :]).then_inc(adj_loaded[t % NS], 16)

            adj_load(0, 0)
            adj_load(0, 1)
            nc.gpsimd.memset(ones[:], 1.0)
            nc.gpsimd.memset(minus_half[:], -0.5)
            nc.gpsimd.memset(eps[:], EPS)
            nc.gpsimd.memset(zero[:], 0.0)
            nc.gpsimd.memset(ident_f[:], 0.0).then_inc(consts_made, 1)
            pool.wait_ge(consts_made, 1)
            nc.gpsimd.affine_select(out=ident_f[:], in_=ident_f[:], compare_op=ALU.not_equal, fill=1.0, base=0,
                                    pattern=[[-1, P]], channel_multiplier=1).then_inc(consts_made, 1)
            pool.wait_ge(consts_made, 2)
            nc.gpsimd.tensor_copy(ident_b[:, 0, :], ident_f[:]).then_inc(consts_made, 1)
            nc.gpsimd.tensor_scalar(ident_b[:, 1, :], ident_f[:], 256.0, None, ALU.mult).then_inc(consts_made, 1)
            pool.wait_ge(consts_made, 4)

            def tile_rstd(n, t):
                j, q = 16 * n + t, t % 8
                pool.wait_ge(moments_made, j + 1)
                wait(pool, h_made, j - 7)
                col = slice(q, q + 1)
                nc.gpsimd.tensor_tensor(vareps[:, col], moment[:, q, 1:2], eps[:], ALU.add).then_inc(rstd_steps, 1)
                pool.wait_ge(rstd_steps, 4 * j + 1)
                nc.gpsimd.tensor_tensor(rstd[:, col], vareps[:, col], minus_half[:], ALU.pow).then_inc(rstd_steps, 1)
                pool.wait_ge(rstd_steps, 4 * j + 2)
                nc.gpsimd.tensor_tensor(scaled[:, col], moment[:, q, 0:1], rstd[:, col],
                                        ALU.mult).then_inc(rstd_steps, 1)
                pool.wait_ge(rstd_steps, 4 * j + 3)
                nc.gpsimd.tensor_tensor(shift[:, col], zero[:], scaled[:, col], ALU.subtract).then_inc(rstd_steps, 1)

            def phase(ph):
                for s in range(STEPS):
                    for graph, t in adj_jobs(ph, s):
                        adj_load(graph, t)
                    if ph.next is not None and s in TILE_AT:
                        tile_rstd(ph.next.p, TILE_AT[s])

            for t in range(T):
                tile_rstd(0, t)
                if t % 4 == 3 and t // 4 + NS < TC:
                    adj_load(0, t // 4 + NS)
            program(pool, phase)

        @block.vector
        def _(dve):
            def edge_weights(ph, c, kt):
                m, i = kt // 2, kt % 2
                if kt == 0:
                    dve.wait_ge(adj_kept, 32 * ph.graph + 8 * c + 8)
                    dve.wait_ge(beta_in_012 if c < NC - 1 else beta_in_3, 16 * (ph.p + 1))
                    dve.wait_ge(factors_made, ph.p + 1)
                if i == 0:
                    wait(dve, g_lo_made, STEPS * ph.p + NQ * c + m - GS + 1)
                byte = adj_t[:, ph.parity, m, CH * c:CH * c + CH].bitcast(U8)[:, i:2 * CH:2]
                nc.vector.scalar_tensor_tensor(
                    out=g_full[:, m % GS, i, :], in0=beta_b[:, CH * c:CH * c + CH],
                    scalar=r_col[:, ph.odd, kt:kt + 1], in1=byte, op0=ALU.max, op1=ALU.mult).then_inc(g_made, 1)

            def edge_weights_ahead(ph, s, i):
                if s + 1 < STEPS:
                    edge_weights(ph, (s + 1) // NQ, 2 * ((s + 1) % NQ) + i)
                elif ph.next is not None:
                    edge_weights(ph.next, 0, i)

            def edge_rest(ph, s):
                k = STEPS * ph.p + s
                dve.wait_ge(g_hi_made, k + 1)
                wait(dve, pair_done, k - GS + 1)
                nc.vector.tensor_tensor(g_lo[:, s % GS, :, :], g_full[:, s % GS, :, :],
                                        g_hi[:, s % GS, :, :].bitcast(F32), ALU.subtract).then_inc(g_lo_made, 1)

            def rows_ready(ph, t):
                if ph.layer == 0:
                    dve.wait_ge(x_loaded[t % XS], 16 * (T // XS * ph.graph + t // XS + 1))
                else:
                    dve.wait_ge(x1_made, 16 * ph.graph + t + 1)
                wait(dve, rstd_steps, 4 * (16 * ph.p + t - 7))

            def tile_stats(ph, t):
                src = x_in[:, t % XS, :] if ph.layer == 0 else xres[:, ph.parity, t, :]
                nc.vector.bn_stats(stat[:, t % 8, :], src).then_inc(stats_made, 1)

            def stats_ready(ph, t):
                dve.wait_ge(stats_made, 16 * ph.p + t + 1)

            def tile_moments(t):
                nc.vector.bn_aggr(moment[:, t % 8, :], stat[:, t % 8, :]).then_inc(moments_made, 1)

            def reduce(n):
                dve.wait_ge(wh_kept, 16 * n + 16)
                nc.vector.tensor_reduce(out=htot[:], in_=hsum[:, :, :], axis=AX, op=ALU.add).then_inc(reduced, 1)
                nc.vector.tensor_reduce(out=fmax[:], in_=wh[:, :, F + 1], axis=AX, op=ALU.max).then_inc(reduced, 1)

            def top(n):
                dve.wait_ge(fmax_turned, n + 1)
                nc.vector.tensor_reduce(out=fmax_top[:], in_=ps_w[0:1, 0:P], axis=AX, op=ALU.max).then_inc(top_made, 1)

            def arguments(n):
                dve.wait_ge(top_spread, n + 1)
                nc.vector.tensor_copy(fmax_all[:], ps_w[:, P:P + 1]).then_inc(fmax_made, 1)
                dve.wait_ge(fmax_made, n + 1)
                nc.vector.tensor_scalar(f2_rel[:], wh[:, :, F + 1], fmax_all[:], FLOOR,
                                        ALU.subtract, ALU.max).then_inc(args_made, 1)
                nc.vector.tensor_scalar(f1_top[:], wh[:, :, F], fmax_all[:], 0.0,
                                        ALU.add, ALU.max).then_inc(args_made, 1)
                dve.wait_ge(args_made, 2 * n + 2)
                nc.vector.memset(wh[:, :, F:F + 1], 1.0).then_inc(one_made, 1)

            def values_rest(n, m):
                pair = slice(2 * m, 2 * m + 2)
                dve.wait_ge(v_hi_made, NQ * n + m + 1)
                nc.vector.tensor_tensor(v_lo[:, pair, 0:FV], wh[:, pair, 0:FV], v_hi[:, pair, 0:FV].bitcast(F32),
                                        ALU.subtract).then_inc(v_lo_made, 1)

            def end_shift(ph, c):
                return 2 if ph.layer == 0 and c == NC - 1 else 0

            def chunk_ready(ph, c, q):
                if q == 2 + end_shift(ph, c):
                    dve.wait_ge(fix_steps, 3 * (NC * ph.p + c) + 1)
                    dve.wait_ge(mean_kept, ph.p + 1)

            def chunk_end(ph, c, q):
                k = NC * ph.p + c
                q -= end_shift(ph, c)
                if q == 1:
                    dve.wait_ge(acc_kept, 4 * k + 4)
                    nc.vector.tensor_scalar(alone[:], acc_sb[:, :, F + 1], 0.0, None,
                                            ALU.is_equal).then_inc(fix_steps, 1)
                if q == 2:
                    nc.vector.copy_predicated(
                        acc_sb[:, :, 0:FV], alone[:].unsqueeze(2).broadcast_to([P, TC, FV]),
                        wh_mean[:, ph.odd, :].unsqueeze(1).broadcast_to([P, TC, FV])).then_inc(fix_steps, 1)
                if q == 3:
                    dve.wait_ge(fix_steps, 3 * k + 2)
                    nc.vector.reciprocal(rden[:], acc_sb[:, :, F]).then_inc(fix_steps, 1)
                if q in (4, 5) and ph.layer == 0:
                    if q == 4:
                        dve.wait_ge(fix_steps, 3 * k + 3)
                        dve.wait_ge(res_loaded[c], 16 * (ph.graph + 1))
                    for t in (2 * q - 8, 2 * q - 7):
                        row = xres[:, ph.parity, TC * c + t, :]
                        nc.vector.scalar_tensor_tensor(out=row, in0=acc_sb[:, t, 0:F], scalar=rden[:, t:t + 1],
                                                       in1=row, op0=ALU.mult, op1=ALU.add).then_inc(x1_made, 1)
                if q in (5, 7) and ph.layer == 1:
                    lot = (q - 5, q - 4)
                    j = 16 * ph.graph + 4 * c
                    for t in lot:
                        dve.wait_ge(elu_parts, j + t + 1)
                        e = expy[:, t % 2, :]
                        nc.vector.scalar_tensor_tensor(out=e, in0=e, scalar=1.0, in1=acc_sb[:, t, 0:F],
                                                       op0=ALU.min, op1=ALU.add).then_inc(elu_half, 1)
                    for t in lot:
                        dve.wait_ge(elu_half, j + t + 1)
                        row = xres[:, ph.parity, TC * c + t, :]
                        nc.vector.scalar_tensor_tensor(out=row, in0=expy[:, t % 2, :], scalar=-1.0, in1=row,
                                                       op0=ALU.add, op1=ALU.add).then_inc(out_made, 1)

            def phase(ph):
                for s in range(STEPS):
                    c, q = s // NQ, s % NQ
                    late, at = before(ph, c)
                    if late is not None:
                        chunk_ready(late, at, q)
                    has_tile = ph.next is not None and s + 1 in TILE_AT
                    if has_tile:
                        rows_ready(ph.next, TILE_AT[s + 1])
                    edge_weights_ahead(ph, s, 0)
                    if has_tile:
                        tile_stats(ph.next, TILE_AT[s + 1])
                    edge_weights_ahead(ph, s, 1)
                    if has_tile:
                        stats_ready(ph.next, TILE_AT[s + 1])
                    edge_rest(ph, s)
                    if has_tile:
                        tile_moments(TILE_AT[s + 1])
                    if late is not None:
                        chunk_end(late, at, q)
                    if s < REST_AT + NQ - STEPS:
                        values_rest(ph.p, STEPS - REST_AT + s)
                    if ph.next is not None:
                        if s == REDUCE_AT:
                            reduce(ph.next.p)
                        if s == FACTOR_AT:
                            top(ph.next.p)
                        if s == FACTOR_AT + 1:
                            arguments(ph.next.p)
                        if s >= REST_AT:
                            values_rest(ph.next.p, s - REST_AT)

            def weight_columns():
                dve.wait_ge(setup_dma, 64)
                for n in range(2):
                    for k in range(K2):
                        for i in range(2):
                            ins = nc.vector.tensor_tensor_reduce(
                                out=g_full[:, 1, n, F * i:F * i + F], in0=wcat[:, n, k, 0:F],
                                in1=g_full[:, 0, n, F * i:F * i + F], scale=1.0, scalar=0.0, op0=ALU.mult, op1=ALU.add,
                                accum_out=wcat[:, n, k, F + i:F + i + 1])
                            ins.then_inc(wcat_made, 1)
                            dve.wait_ge(wcat_made, 4 * n + 2 * k + i + 1)
                nc.vector.memset(v_hi[:, :, F + 1:F + 2].bitcast(F32), 1.0)
                nc.vector.memset(v_lo[:, :, F + 1:F + 2].bitcast(F32), 0.0)
                nc.vector.memset(wh_mean[:, :, F:F + 1], 1.0).then_inc(vconst_made, 1)
                dve.wait_ge(vconst_made, 1)

            first = opening()[0]
            for t in range(T + 1):
                if t < T:
                    rows_ready(first, t)
                    tile_stats(first, t)
                if t:
                    stats_ready(first, t - 1)
                    tile_moments(t - 1)
                if t == XS - 1:
                    weight_columns()
            reduce(0)
            top(0)
            arguments(0)
            for m in range(STEPS - REST_AT):
                values_rest(0, m)
            for i in range(2):
                edge_weights(first, 0, i)
            program(dve, phase)
            last = closing()[1]
            for q in range(NQ):
                chunk_ready(last, NC - 1, q)
                chunk_end(last, NC - 1, q)

        @block.scalar
        def _(act):
            def adj_keep(graph, t, halves=(0, 1)):
                j = 16 * graph + t
                for h in halves:
                    act.wait_ge(adj_turned, 2 * j + h + 1)
                    nc.scalar.activation(adj_t[:, graph % 2, NQ // 2 * h:NQ // 2 * (h + 1), P * t:P * t + P],
                                         ps_a[h][:, :, :],
                                         ACT.Copy).then_inc(adj_kept, 1)

            def tile_normalise(ph, t):
                j, q = 16 * ph.p + t, t % 8
                act.wait_ge(rstd_steps, 4 * j + 4)
                wait(act, h_turned, j - 1)
                src = x_in[:, t % XS, :] if ph.layer == 0 else xres[:, ph.parity, t, :]
                nc.scalar.activation(hrow[:, t % 2, :], src, ACT.Relu, bias=shift[:, q:q + 1],
                                     scale=rstd[:, q:q + 1]).then_inc(h_made, 1)

            def tile_columns(ph, t, lead=0):
                j = 16 * ph.p + t
                source, place = (lead_h[t % 2], lead_col[t % 2]) if lead else (ps_h, hcol)
                act.wait_ge(h_turned, j + 1)
                wait(act, wh_done, j - lead)
                if t == 0:
                    wait(act, reduced, 2 * ph.p)
                for k in range(K2):
                    ins = nc.scalar.activation(place[:, k, :], source[:, k, 0:P], ACT.Copy,
                                               accum_out=hsum[:, k, t:t + 1])
                ins.then_inc(hcol_made, 1)

            def tile_keep(ph, t, lead=0):
                j = 16 * ph.p + t
                source = lead_w[t % 2] if lead else ps_w
                act.wait_ge(wh_done, j + 1)
                wait(act, v_lo_made, NQ * (ph.p - 1) + t // 2 + 1)
                nc.scalar.activation(wh[:, t, :], source[:, 0:FW], ACT.Copy).then_inc(wh_kept, 1)

            def factors(ph):
                n = ph.p
                act.wait_ge(args_made, 2 * n + 2)
                nc.scalar.activation(r_col[:, ph.odd, :], f2_rel[:], ACT.Exp, scale=1.0 - SLOPE)
                nc.scalar.activation(v_col[:], f2_rel[:], ACT.Exp, scale=SLOPE)
                nc.scalar.activation(beta_c[:], f1_top[:], ACT.Exp, scale=SLOPE - 1.0).then_inc(factors_made, 1)
                act.wait_ge(reduced, 2 * n + 2)
                for k in range(K2):
                    ins = nc.scalar.activation(hmean_b[:, k, :], ones[:], ACT.Copy, scale=htot[:, k:k + 1])
                ins.then_inc(hmean_made, 1)

            def spread(ph):
                n = ph.p
                act.wait_ge(beta_turned, n + 1)
                wait(act, beta_stored, 16 * n)
                nc.scalar.activation(beta_r[:], ps_w[0:T, 0:P], ACT.Copy).then_inc(beta_kept, 1)
                act.wait_ge(mean_done, n + 1)
                nc.scalar.activation(wh_mean[:, ph.odd, 0:F], ps_h[:, 0, 0:F], ACT.Copy,
                                     scale=1.0 / N).then_inc(mean_kept, 1)

            def values_high(n, m):
                act.wait_ge(one_made, n + 1)
                act.wait_ge(factors_made, n + 1)
                wait(act, pair_done, STEPS * (n - 1) + 3 * NQ + m + 1)
                for kt in (2 * m, 2 * m + 1):
                    ins = nc.scalar.activation(wh[:, kt, 0:FV], wh[:, kt, 0:FV], ACT.Copy,
                                               scale=v_col[:, kt:kt + 1])
                ins.then_inc(v_made, 1)
                act.wait_ge(v_made, NQ * n + m + 1)
                nc.scalar.activation(v_hi[:, 2 * m:2 * m + 2, 0:FV], wh[:, 2 * m:2 * m + 2, 0:FV],
                                     ACT.Copy).then_inc(v_hi_made, 1)

            def edge_high(ph, s):
                k = STEPS * ph.p + s
                act.wait_ge(g_made, 2 * k + 2)
                wait(act, pair_done, k - GS + 1)
                nc.scalar.activation(g_hi[:, s % GS, :, :], g_full[:, s % GS, :, :], ACT.Copy).then_inc(g_hi_made, 1)

            def edge_high_ahead(ph, s):
                if s + 1 < STEPS:
                    edge_high(ph, s + 1)
                elif ph.next is not None:
                    edge_high(ph.next, 0)

            def acc_keep(ph, c):
                k = NC * ph.p + c
                late, at = before(ph, c)
                if late is not None:
                    act.wait_ge(out_made if late.layer else x1_made, 16 * late.graph + 4 * at + 4)
                for t in range(TC):
                    if t < TC - 1:
                        act.wait_ge(acc_done, 3 * k + t + 1)
                    else:
                        act.wait_ge(pair_done, NQ * (k + 1))
                    nc.scalar.activation(acc_sb[:, t, :], acc[t][:, 0:FW], ACT.Copy).then_inc(acc_kept, 1)

            def elu(ph, c, q):
                k = NC * ph.p + c
                j = 16 * ph.graph + 4 * c
                act.wait_ge(fix_steps, 3 * k + 3)
                for t in (q - 3, q - 2):
                    if t >= 2:
                        act.wait_ge(out_made, j + t - 1)
                    nc.scalar.activation(expy[:, t % 2, :], acc_sb[:, t, 0:F], ACT.Exp, scale=rden[:, t:t + 1])
                    nc.scalar.activation(acc_sb[:, t, 0:F], acc_sb[:, t, 0:F], ACT.Relu,
                                         scale=rden[:, t:t + 1]).then_inc(elu_parts, 1)

            def phase(ph):
                for s in range(STEPS):
                    c, q = s // NQ, s % NQ
                    late, at = before(ph, c)
                    if q == 0 and late is not None:
                        acc_keep(late, at)
                    edge_high_ahead(ph, s)
                    for graph, t in adj_jobs(ph, s - 1):
                        adj_keep(graph, t, (1,))
                    if ph.next is not None:
                        if s - 3 in TILE_AT:
                            tile_keep(ph.next, TILE_AT[s - 3])
                        if s - 2 in TILE_AT:
                            tile_columns(ph.next, TILE_AT[s - 2])
                        if s in TILE_AT:
                            tile_normalise(ph.next, TILE_AT[s])
                    if late is not None and late.layer == 1 and q in (3, 5):
                        elu(late, at, q)
                    if s < HIGH_AT + NQ - STEPS:
                        values_high(ph.p, STEPS - HIGH_AT + s)
                    if ph.next is not None:
                        if s == EXP_AT:
                            factors(ph.next)
                        if s == SPREAD_AT:
                            spread(ph.next)
                        if s >= HIGH_AT:
                            values_high(ph.next.p, s - HIGH_AT)
                    for graph, t in adj_jobs(ph, s):
                        adj_keep(graph, t, (0,))

            first = opening()[0]
            for t in range(T + 2):
                if t < T:
                    tile_normalise(first, t)
                if 1 <= t <= T:
                    tile_columns(first, t - 1, 1)
                if t >= 2:
                    tile_keep(first, t - 2, 1)
                if t % 4 == 1 and t < T:
                    adj_keep(0, t // 4)
            factors(first)
            spread(first)
            for m in range(STEPS - HIGH_AT):
                values_high(0, m)
            edge_high(first, 0)
            program(act, phase)
            last = closing()[1]
            acc_keep(last, NC - 1)
            for q in (3, 5):
                elu(last, NC - 1, q)

        @block.tensor
        def _(pe):
            def adj_turn(graph, t, h):
                j = 16 * graph + t
                if h == 0:
                    pe.wait_ge(adj_loaded[t % NS], 16 * (8 * graph + t // 2 + 1))
                wait(pe, adj_kept, 2 * j + h - 1)
                for m in range(NQ // 2):
                    for i in range(2):
                        kt = NQ * h + 2 * m + i
                        ins = nc.tensor.matmul(ps_a[h][:, m, :], adj_in[:, t % NS, P * kt:P * kt + P],
                                               ident_b[:, i, :], start=(i == 0), stop=(i == 1))
                ins.then_inc(adj_turned, 1)

            def tile_turn(n, t, lead=0):
                j = 16 * n + t
                bank = lead_h[t % 2] if lead else ps_h
                pe.wait_ge(h_made, j + 1)
                wait(pe, hcol_made, j - lead)
                if t == 0:
                    wait(pe, mean_kept, n)
                for k in range(K2):
                    ins = nc.tensor.transpose(bank[:, k, 0:P], hrow[:, t % 2, P * k:P * k + P], ident_f[:])
                ins.then_inc(h_turned, 1)

            def tile_project(ph, t, lead=0):
                n = ph.p
                bank, rows = (lead_w[t % 2], lead_col[t % 2]) if lead else (ps_w, hcol)
                j = 16 * n + t
                pe.wait_ge(hcol_made, j + 1)
                wait(pe, wh_kept, j - lead)
                if t == 0:
                    wait(pe, beta_kept, n)
                for k in range(K2):
                    ins = nc.tensor.matmul(bank[:, 0:FW], rows[:, k, :], wcat[:, ph.layer, k, :],
                                           start=(k == 0), stop=(k == K2 - 1))
                ins.then_inc(wh_done, 1)

            def maximum_turn(n):
                pe.wait_ge(reduced, 2 * n + 2)
                nc.tensor.transpose(ps_w[0:1, 0:P], fmax[:], ident_f[:]).then_inc(fmax_turned, 1)

            def maximum_spread(n):
                pe.wait_ge(top_made, n + 1)
                nc.tensor.matmul(ps_w[:, P:P + 1], ones[0:1, :], fmax_top[:], start=True,
                                 stop=True).then_inc(top_spread, 1)

            def spread(ph):
                n = ph.p
                pe.wait_ge(factors_made, n + 1)
                pe.wait_ge(wh_kept, 16 * n + 16)
                nc.tensor.transpose(ps_w[0:T, 0:P], beta_c[:], ident_f[:]).then_inc(beta_turned, 1)
                pe.wait_ge(hmean_made, n + 1)
                for k in range(K2):
                    ins = nc.tensor.matmul(ps_h[:, 0, 0:F], hmean_b[:, k, :], wcat[:, ph.layer, k, 0:F],
                                           start=(k == 0), stop=(k == K2 - 1))
                ins.then_inc(mean_done, 1)

            def attend(ph, s, i):
                c, q = s // NQ, s % NQ
                kt = 2 * q + i
                if i == 0:
                    pe.wait_ge(g_lo_made, STEPS * ph.p + s + 1)
                    if c == 0:
                        pe.wait_ge(v_lo_made, NQ * ph.p + q + 1)
                for t in range(TC):
                    if kt == 0:
                        wait(pe, acc_kept, 4 * (NC * ph.p + c) + t - 3)
                    hi = g_hi[:, q % GS, i, P * t:P * t + P]
                    lo = g_lo[:, q % GS, i, P * t:P * t + P]
                    nc.tensor.matmul(acc[t][:, 0:FW], hi, v_hi[:, kt, :], start=(kt == 0), stop=False)
                    nc.tensor.matmul(acc[t][:, 0:FW], hi, v_lo[:, kt, :], start=False, stop=False)
                    ins = nc.tensor.matmul(acc[t][:, 0:FW], lo, v_hi[:, kt, :], start=False, stop=(kt == T - 1))
                    if kt == T - 1 and t < TC - 1:
                        ins.then_inc(acc_done, 1)
                if i == 1:
                    ins.then_inc(pair_done, 1)

            def phase(ph):
                for s in range(STEPS):
                    for i in range(2):
                        attend(ph, s, i)
                        for graph, t in adj_jobs(ph, s):
                            adj_turn(graph, t, i)
                    if ph.next is not None and s - 2 in TILE_AT:
                        tile_project(ph.next, TILE_AT[s - 2])
                    if ph.next is not None and s - 1 in TILE_AT:
                        tile_turn(ph.next.p, TILE_AT[s - 1])
                    if ph.next is not None:
                        if s == REDUCE_AT:
                            maximum_turn(ph.next.p)
                        if s == FACTOR_AT:
                            maximum_spread(ph.next.p)
                        if s == EXP_AT:
                            spread(ph.next)

            pe.wait_ge(consts_made, 4)
            first = opening()[0]
            for t in range(T + 1):
                if t < T:
                    tile_turn(0, t, 1)
                if t == 1:
                    pe.wait_ge(wcat_made, 4)
                if t:
                    tile_project(first, t - 1, 1)
                if t % 4 == 1 and t < T:
                    adj_turn(0, t // 4, 0)
                    adj_turn(0, t // 4, 1)
            pe.wait_ge(wcat_made, 8)
            pe.wait_ge(vconst_made, 1)
            maximum_turn(0)
            maximum_spread(0)
            spread(first)
            program(pe, phase)


_INS = ["x", "adj", "L0_gnn_W", "L0_gnn_a", "L1_gnn_W", "L1_gnn_a"]


def kernel(**inputs):
    import numpy as np
    import concourse.bacc as bacc
    from concourse.bass_utils import run_bass_kernel_spmd

    nc = bacc.Bacc("TRN2", target_bir_lowering=False, num_devices=1)
    arrays, args = {}, []
    for name in _INS:
        a = np.ascontiguousarray(inputs[name])
        if name.endswith("_a"):
            a = a.reshape(-1)
        arrays[f"in_{name}"] = a
        args.append(nc.dram_tensor(f"in_{name}", a.shape, mybir.dt.from_np(a.dtype), kind="ExternalInput").ap())
    shape = arrays["in_x"].shape
    args.append(nc.dram_tensor("out_x", shape, F32, kind="ExternalOutput").ap())
    gat_kernel(nc, *args)
    r = run_bass_kernel_spmd(nc, [arrays], core_ids=[0])
    return r.results[0]["out_x"]
```
